# Optimizing a Trainium2 kernel written in Bass

```python
import numpy as np
import jax
import jax.numpy as jnp

def _softmax(x, axis=-1):
    return jax.nn.softmax(x, axis=axis)

def _gelu(x):
    return jax.nn.gelu(x, approximate=True)

def _silu(x):
    return jax.nn.silu(x)

def _sigmoid(x):
    return jax.nn.sigmoid(x)

def _layernorm(x, axis=-1, eps=1e-05):
    m = jnp.mean(x, axis=axis, keepdims=True)
    v = jnp.var(x, axis=axis, keepdims=True)
    return (x - m) / jnp.sqrt(v + eps)

def _scatter_add(tgt, idx, src, axis=0):
    return tgt.at[idx].add(src)

def _segment_sum(src, seg, n):
    return jax.ops.segment_sum(src, seg, n)
kernel_name = 'mk_hybrid_d1_jaxref_r8_ef69be'

def setup_inputs(seed: int=0):
    np.random.seed(seed)
    _w = jnp.asarray

    def _L0_attn_a_setup():
        import jax, jax.numpy as jnp
        import numpy as np
        NUM_HEADS = 32
        HIDDEN = 256
        HEAD_DIM = HIDDEN // NUM_HEADS
        BATCH = 2
        SEQ = 256
        STD = 0.02

        def _split_heads(x):
            b, s, _ = x.shape
            return x.reshape(b, s, NUM_HEADS, HEAD_DIM).transpose(0, 2, 1, 3)
        key = jax.random.key(seed)
        ks = jax.random.split(key, 9)

        def w(k):
            return jax.random.normal(k, (HIDDEN, HIDDEN), dtype=jnp.float32) * STD
        return {'hidden_states': jax.random.normal(ks[0], (BATCH, SEQ, HIDDEN), dtype=jnp.float32), 'Wq': w(ks[1]), 'bq': jnp.zeros((HIDDEN,), jnp.float32), 'Wk': w(ks[2]), 'bk': jnp.zeros((HIDDEN,), jnp.float32), 'Wv': w(ks[3]), 'bv': jnp.zeros((HIDDEN,), jnp.float32), 'Wo': w(ks[4]), 'bo': jnp.zeros((HIDDEN,), jnp.float32)}
    _L0_attn_a_in = _L0_attn_a_setup()

    def _L0_attn_b_setup():
        import jax, jax.numpy as jnp
        import numpy as np
        B, L, D = (2, 256, 256)
        H, HK = (32, 8)
        HD = D // H
        W = 128
        key = jax.random.key(seed)
        ks = jax.random.split(key, 5)
        s = 1.0 / np.sqrt(D).astype(np.float32)
        return {'x': jax.random.normal(ks[0], (B, L, D), jnp.float32), 'wq': jax.random.normal(ks[1], (D, D), jnp.float32) * s, 'wk': jax.random.normal(ks[2], (D, HK * HD), jnp.float32) * s, 'wv': jax.random.normal(ks[3], (D, HK * HD), jnp.float32) * s, 'wo': jax.random.normal(ks[4], (D, D), jnp.float32) * s}
    _L0_attn_b_in = _L0_attn_b_setup()

    def _L0_ffn_setup():
        import jax, jax.numpy as jnp
        import numpy as np

        def _sparsify_2to4(h):
            B, S, I = h.shape
            g = h.reshape(B, S, I // 4, 4)
            a = jnp.abs(g)
            _, idx = jax.lax.top_k(a, 2)
            pos = jnp.arange(4)
            mask = (pos == idx[..., 0:1]) | (pos == idx[..., 1:2])
            return (g * mask.astype(g.dtype)).reshape(B, S, I)
        key = jax.random.key(seed)
        k1, k2, k3, k4 = jax.random.split(key, 4)
        B, S, H, I = (4, 256, 256, 1024)
        x = jax.random.normal(k1, (B, S, H), dtype=jnp.float32)
        w_gate = jax.random.normal(k2, (H, I), dtype=jnp.float32) / np.sqrt(H)
        w_up = jax.random.normal(k3, (H, I), dtype=jnp.float32) / np.sqrt(H)
        w_down = jax.random.normal(k4, (I, H), dtype=jnp.float32) / np.sqrt(I)
        return {'x': x, 'w_gate': w_gate, 'w_up': w_up, 'w_down': w_down}
    _L0_ffn_in = _L0_ffn_setup()
    _d = {'L0_attn_a_hidden_states': _L0_attn_a_in['hidden_states'], 'L0_attn_a_Wq': _L0_attn_a_in['Wq'], 'L0_attn_a_bq': _L0_attn_a_in['bq'], 'L0_attn_a_Wk': _L0_attn_a_in['Wk'], 'L0_attn_a_bk': _L0_attn_a_in['bk'], 'L0_attn_a_Wv': _L0_attn_a_in['Wv'], 'L0_attn_a_bv': _L0_attn_a_in['bv'], 'L0_attn_a_Wo': _L0_attn_a_in['Wo'], 'L0_attn_a_bo': _L0_attn_a_in['bo'], 'L0_attn_b_wq': _L0_attn_b_in['wq'], 'L0_attn_b_wk': _L0_attn_b_in['wk'], 'L0_attn_b_wv': _L0_attn_b_in['wv'], 'L0_attn_b_wo': _L0_attn_b_in['wo'], 'L0_ffn_w_gate': _L0_ffn_in['w_gate'], 'L0_ffn_w_up': _L0_ffn_in['w_up'], 'L0_ffn_w_down': _L0_ffn_in['w_down']}
    _x0 = _d['L0_attn_a_hidden_states']
    _d['L0_attn_a_hidden_states'] = jax.random.normal(jax.random.fold_in(jax.random.key(seed), 1), (2, 1024, 256), dtype=_x0.dtype)
    del _x0
    return _d

def reference(L0_attn_a_hidden_states, L0_attn_a_Wq, L0_attn_a_bq, L0_attn_a_Wk, L0_attn_a_bk, L0_attn_a_Wv, L0_attn_a_bv, L0_attn_a_Wo, L0_attn_a_bo, L0_attn_b_wq, L0_attn_b_wk, L0_attn_b_wv, L0_attn_b_wo, L0_ffn_w_gate, L0_ffn_w_up, L0_ffn_w_down):

    def _L0_attn_a_ref(hidden_states, Wq, bq, Wk, bk, Wv, bv, Wo, bo):
        import jax, jax.numpy as jnp
        import numpy as np
        NUM_HEADS = 32
        HIDDEN = 256
        HEAD_DIM = HIDDEN // NUM_HEADS
        BATCH = 2
        SEQ = 256
        STD = 0.02

        def _split_heads(x):
            b, s, _ = x.shape
            return x.reshape(b, s, NUM_HEADS, HEAD_DIM).transpose(0, 2, 1, 3)
        scale = 1.0 / jnp.sqrt(jnp.float32(HEAD_DIM))
        q = _split_heads(hidden_states @ Wq + bq)
        k = _split_heads(hidden_states @ Wk + bk)
        v = _split_heads(hidden_states @ Wv + bv)
        scores = jnp.einsum('bhqd,bhkd->bhqk', q, k) * scale
        probs = jax.nn.softmax(scores, axis=-1)
        ctx = jnp.einsum('bhqk,bhkd->bhqd', probs, v)
        b, h, s, d = ctx.shape
        ctx = ctx.transpose(0, 2, 1, 3).reshape(b, s, h * d)
        return ctx @ Wo + bo

    def _L0_attn_b_ref(x, wq, wk, wv, wo):
        import jax, jax.numpy as jnp
        import numpy as np
        B, L, D = (2, 256, 256)
        H, HK = (32, 8)
        HD = D // H
        W = 128
        Bb, Ll, Dm = x.shape
        n_rep = H // HK
        q = (x @ wq).reshape(Bb, Ll, H, HD).transpose(0, 2, 1, 3)
        k = jnp.repeat((x @ wk).reshape(Bb, Ll, HK, HD), n_rep, axis=2).transpose(0, 2, 1, 3)
        v = jnp.repeat((x @ wv).reshape(Bb, Ll, HK, HD), n_rep, axis=2).transpose(0, 2, 1, 3)
        scores = jnp.einsum('bhqd,bhkd->bhqk', q, k) / jnp.float32(np.sqrt(HD))
        i = jnp.arange(Ll)[:, None]
        j = jnp.arange(Ll)[None, :]
        amask = jnp.where((j >= i - W) & (j < i), jnp.float32(-10000000000.0), jnp.float32(0.0))
        attn = jax.nn.softmax(scores + amask[None, None, :, :], axis=-1)
        out = jnp.einsum('bhqk,bhkd->bqhd', attn, v).reshape(Bb, Ll, Dm)
        return out @ wo

    def _L0_ffn_ref(x, w_gate, w_up, w_down):
        import jax, jax.numpy as jnp
        import numpy as np

        def _sparsify_2to4(h):
            B, S, I = h.shape
            g = h.reshape(B, S, I // 4, 4)
            a = jnp.abs(g)
            _, idx = jax.lax.top_k(a, 2)
            pos = jnp.arange(4)
            mask = (pos == idx[..., 0:1]) | (pos == idx[..., 1:2])
            return (g * mask.astype(g.dtype)).reshape(B, S, I)
        h = jax.nn.silu(jnp.einsum('bsh,hi->bsi', x, w_gate)) * jnp.einsum('bsh,hi->bsi', x, w_up)
        h_sparse = _sparsify_2to4(h)
        return jnp.einsum('bsi,ih->bsh', h_sparse, w_down)
    x = L0_attn_a_hidden_states
    x = x + _L0_attn_a_ref(_layernorm(x, axis=-1), L0_attn_a_Wq, L0_attn_a_bq, L0_attn_a_Wk, L0_attn_a_bk, L0_attn_a_Wv, L0_attn_a_bv, L0_attn_a_Wo, L0_attn_a_bo)
    x = x + _L0_ffn_ref(_layernorm(x, axis=-1), L0_ffn_w_gate, L0_ffn_w_up, L0_ffn_w_down)
    x = x + _L0_attn_b_ref(_layernorm(x, axis=-1), L0_attn_b_wq, L0_attn_b_wk, L0_attn_b_wv, L0_attn_b_wo)
    x = x + _L0_ffn_ref(_layernorm(x, axis=-1), L0_ffn_w_gate, L0_ffn_w_up, L0_ffn_w_down)
    return x

_drawn_inputs = setup_inputs


def setup_inputs(seed=0):
    import zlib

    import numpy as np

    out = dict(_drawn_inputs(seed))
    spreads = {'L0_attn_a_bq': (0.0, 0.8),
     'L0_attn_a_bk': (0.0, 0.8),
     'L0_attn_a_bv': (0.0, 0.1),
     'L0_attn_a_bo': (0.0, 0.1)}
    factors = {'L0_attn_a_Wq': 8.0, 'L0_attn_a_Wk': 7.761, 'L0_attn_a_Wv': 4.059}
    for name, (base, spread) in spreads.items():
        noise = np.random.default_rng([zlib.crc32(name.encode()), seed]).standard_normal(out[name].shape)
        drawn = base * np.exp(spread * noise) if base else spread * noise
        out[name] = jnp.asarray(drawn.astype(out[name].dtype))
    for name, factor in factors.items():
        out[name] = (out[name] * factor).astype(out[name].dtype)
    return out
```

```python
from contextlib import ExitStack

import concourse.bass as bass
from concourse import mybir

F32 = mybir.dt.float32
BF16 = mybir.dt.bfloat16
ALU = mybir.AluOpType
ACT = mybir.ActivationFunctionType
AX = mybir.AxisListType

P = 128
BATCH, SEQ, D = 2, 1024, 256
TOKENS = BATCH * SEQ
TILES = TOKENS // P
BT = SEQ // P
DK = D // P
HEADS, HD = 32, 8
KV_HEADS = 8
WINDOW = 128
MASK = -10000000000.0
SCALE = 1.0 / float(HD) ** 0.5
EPS = 1e-5
INNER = 1024
BANK = 512
HALF = SEQ // BANK

GH = 4
GPB = HEADS // GH
GROUPS = BATCH * GPB
PARTS = 3
Q_PART = (0, 0, 1, 1, 0, 2)
K_PART = (0, 1, 0, 1, 2, 0)
ROWS = HD * len(Q_PART)
MROW = ROWS + 8
PAR = 64
UNITS = HALF * BT
CHUNKS = GH * BT
CPH = CHUNKS // HALF
PRING = 4
VW = 32


def masked_blocks(unit):
    qh, kt = divmod(unit, BT)
    return [(kind, kt + kind - qh * (BANK // P)) for kind in (0, 1)
            if kt + kind < BT and (kt + kind) // (BANK // P) == qh]


MASKED_UNITS = [u for u in range(UNITS) if masked_blocks(u)]
MPG = len(MASKED_UNITS)


def hybrid_kernel(nc, x_in, wq_a, bq_a, wk_a, bk_a, wv_a, bv_a, wo_a, bo_a,
                  wq_b, wk_b, wv_b, wo_b, w_gate, w_up, w_down, out):
    ctx = ExitStack()
    with ctx:
        def sb(name, shape, dt=F32):
            return ctx.enter_context(nc.sbuf_tensor(name, shape, dt))

        def sem(name):
            return ctx.enter_context(nc.semaphore(name))

        def dram(name, shape, dt):
            return nc.dram_tensor(name, shape, dt, kind="Internal").ap()

        q_stacks = dram("q_stacks", (GROUPS, GH, ROWS, SEQ), BF16)
        k_stacks = dram("k_stacks", (GROUPS, GH, ROWS, SEQ), BF16)
        k_stacks_b = dram("k_stacks_b", (GROUPS, ROWS, SEQ), BF16)
        q_stacks_b = dram("q_stacks_b", (GROUPS, GH, ROWS, SEQ), BF16)
        max_rows = dram("max_rows", (2, HALF, 2, PARTS, GH // 2 * BANK), BF16)
        ctx_rows = [dram(f"ctx_rows{a}", (GROUPS, GH, VW, SEQ), F32) for a in range(2)]
        inv_rows = [dram(f"inv_rows{a}", (BATCH, HEADS, SEQ), F32) for a in range(2)]

        x = sb("x", [P, TILES, D])
        xn = sb("xn", [P, BT, D])
        xnT = sb("xnT", [P, DK, TOKENS])
        stats = sb("stats", [P, BT, 6])
        mv = sb("mv", [P, BT, 2])
        std = sb("std", [P, BT])
        rstd = sb("rstd", [P, BT])
        eps = sb("eps", [P, 1])
        ident = sb("ident", [P, P])
        ident_bf = sb("ident_bf", [P, P], BF16)
        wqkvo = [sb(f"wqkvo{i}", [P, DK, D]) for i in range(4)]
        wqo_b = [sb(f"wqo_b{i}", [P, DK, D]) for i in range(2)]
        wkv_b = [sb(f"wkv_b{i}", [P, DK, KV_HEADS * HD]) for i in range(2)]
        wg = sb("wg", [P, DK, INNER])
        wu = sb("wu", [P, DK, INNER])
        wd = sb("wd", [P, INNER // P, D])
        bqk = sb("bqk", [P, 2, DK])
        bv_rows = sb("bv_rows", [P, D])
        bo_rows = sb("bo_rows", [P, D])
        band = sb("band", [P, 2, 2 * P])
        band_out = sb("band_out", [P, 2, 2 * P])
        vsb = sb("vsb", [P, GROUPS, BT, GH * HD])
        mneg = sb("mneg", [P, HALF, CPH])
        mband = sb("mband", [P, HALF, CPH])
        mrest = sb("mrest", [P, HALF, CPH])
        mres1 = sb("mres1", [P, HALF, CPH])
        mres2 = sb("mres2", [P, HALF, CPH])
        nought = sb("nought", [P, HALF, CPH])
        mparts = sb("mparts", [P, HALF, 2, PARTS, CPH // 2], BF16)
        mT = sb("mT", [CPH * PARTS, HALF, P], BF16)
        sums = sb("sums", [P, BATCH, 2 * P])
        isums = sb("isums", [P, BATCH, 2 * P])
        area = sb("area", [P, 24576])
        top = [0]

        def carve(n_bytes, shape, dt):
            size = 4 if dt == F32 else 2
            n = 1
            for s in shape:
                n *= s
            a = top[0]
            top[0] += n * size // 4
            v = area[:, a:top[0]]
            if dt != F32:
                v = v.bitcast(dt)
            names = "abcd"[:len(shape)]
            return v.rearrange("p (" + " ".join(names) + ") -> p " + " ".join(names),
                               **{names[i]: shape[i] for i in range(len(shape))})

        q_max, q_st = (carve(0, [2, GH, SEQ], BF16) for _ in range(2))
        k_max, k_st = (carve(0, [2, GH // 2, SEQ], BF16) for _ in range(2))
        vaug = carve(0, [2, BT, GH, VW], F32)
        probs = carve(0, [PRING, GH, BANK], F32)
        ctx_sb = carve(0, [HALF, BANK], F32)
        parts = ctx_top = None
        attention_top = top[0]
        top[0] = attention_top - HALF * BANK - PRING * GH * BANK
        parts = carve(0, [2, PARTS, SEQ], BF16)
        resid = carve(0, [2, BANK], F32)
        top[0] = attention_top - HALF * BANK - PRING * GH * BANK
        ctxn = carve(0, [2, DK, BANK], F32)
        inv = carve(0, [2, DK, BANK], F32)
        top[0] = 0
        hid = carve(0, [2, INNER // P, BANK], F32)
        gated = carve(0, [2, BANK], F32)
        mag = carve(0, [4, BANK], F32)
        wins = carve(0, [6, BANK], BF16)
        tally = carve(0, [4, BANK], BF16)
        tally2 = carve(0, [4, BANK], BF16)
        assert top[0] <= 24576 and attention_top <= 24576, (top[0], attention_top)

        psum = ctx.enter_context(nc.psum_tensor("psum", [P, 8, BANK], F32))
        T_BANK = psum[:, 7, :].bitcast(BF16)
        PV_BANK = 6

        x_loaded = [sem(f"x_loaded{b}") for b in range(BATCH)]
        w_loaded = [sem("wa_loaded"), sem("wb_loaded")]
        wf_loaded = sem("wf_loaded")
        bias_loaded = sem("bias_loaded")
        stacks_stored = sem("stacks_stored")
        max_loaded = [sem(f"max_stack_loaded{i}") for i in range(2)]
        st_loaded = [sem(f"stack_loaded{i}") for i in range(2)]
        mrow_stored = sem("mrow_stored")
        mrow_loaded = sem("mrow_loaded")
        ctx_stored = sem("ctx_stored")
        sums_loaded = sem("sums_loaded")
        inv_stored = sem("inv_stored")
        ctx_loaded = [sem(f"ctx_loaded{i}") for i in range(2)]
        out_stored = sem("out_stored")
        const_ready = sem("const_ready")
        area_set = sem("area_set")
        ln_stats, ln_mv, ln_sd, ln_rstd, ln_xn = (sem(s) for s in ("ln_stats", "ln_mv", "ln_sd", "ln_rstd", "ln_xn"))
        ln_tr, ln_evac = sem("ln_tr"), sem("ln_evac")
        proj_ready, hi_done, rest_done, mid_done, lo_done = (
            sem(s) for s in ("proj_ready", "hi_done", "rest_done", "mid_done", "lo_done"))
        v_ready, v_done = sem("v_ready"), sem("v_done")
        vaug_ready = sem("vaug_ready")
        max_ready, max_used = sem("max_ready"), sem("max_used")
        cols_ready, split_done, mparts_ready = sem("cols_ready"), sem("split_done"), sem("mparts_ready")
        mT_ready, mT_copied = sem("mT_ready"), sem("mT_copied")
        st_ready, exp_done, masked, pv_done, ctx_copied = (
            sem(s) for s in ("st_ready", "exp_done", "masked", "pv_done", "ctx_copied"))
        isums_ready, ctxn_ready, o_ready = sem("isums_ready"), sem("ctxn_ready"), sem("o_ready")
        turn_started, mask_started = sem("turn_started"), sem("mask_started")
        x_biased, x_updated = sem("x_biased"), sem("x_updated")
        gate_ready, up_ready, silu_done, hid_done, mag_done, wins_done, tally_done, tally2_done, sparse_done, down_ready = (
            sem(s) for s in ("gate_ready", "up_ready", "silu_done", "hid_done", "mag_done", "wins_done",
                             "tally_done", "tally2_done", "sparse_done", "down_ready"))

        QUARTERS = [
            [(0, 0, P), (0, 1, P), (1, 0, P), (1, 1, P)],
            [(0, 0, P), (0, 1, P), (1, 0, KV_HEADS * HD)],
        ]
        PCH = [2 * len(q) for q in QUARTERS]
        PBASE = [0, BATCH * PCH[0]]
        VCH = [BT // 2, 1]
        VBASE = [0, BATCH * VCH[0]]
        SD = 16 * len(Q_PART)
        NQ = [len(q) for q in QUARTERS]
        QBASE = [0, BATCH * NQ[0]]
        w_a = [[wqkvo[0], wqkvo[1], wqkvo[2], wqkvo[3]], [wqo_b[0], wkv_b[0], wkv_b[1], wqo_b[1]]]
        STACK_DMAS = 64

        def loads(G, buf):
            return STACK_DMAS // 2 * (G - buf) + STACK_DMAS

        block = ctx.enter_context(nc.Block())

        @block.sync
        def _(sp):
            for b in range(BATCH):
                sp.dma_start(x[:, b * BT:(b + 1) * BT, :],
                             x_in[b].rearrange("(t p) d -> p t d", p=P)).then_inc(x_loaded[b], 16)
            for w, src in zip(wqkvo, (wq_a, wk_a, wv_a, wo_a)):
                sp.dma_start(w[:], src.rearrange("(k p) n -> p k n", p=P)).then_inc(w_loaded[0], 16)
            for i, src in enumerate((bq_a, bk_a)):
                sp.dma_start(bqk[:, i, :], src.rearrange("(m p) -> p m", p=P),
                             allow_slow_non_contiguous=True).then_inc(bias_loaded, 16)
            for dst, src in ((bv_rows, bv_a), (bo_rows, bo_a)):
                sp.dma_start(dst[:], src.rearrange("(o d) -> o d", o=1).to_broadcast((P, D))).then_inc(bias_loaded, 16)
            for w, src in zip((*wqo_b, *wkv_b), (wq_b, wo_b, wk_b, wv_b)):
                sp.dma_start(w[:], src.rearrange("(k p) n -> p k n", p=P)).then_inc(w_loaded[1], 16)
            for w, src in ((wg, w_gate), (wu, w_up)):
                sp.dma_start(w[:], src.rearrange("(k p) n -> p k n", p=P)).then_inc(wf_loaded, 16)
            sp.dma_start(wd[:].rearrange("p (h r) n -> p h r n", h=2),
                         w_down.rearrange("(h p r) n -> p h r n", h=2, r=4)).then_inc(wf_loaded, 16)

            def store_stacks(a, b):
                for j, (w, m, rows) in enumerate(QUARTERS[a]):
                    n = QBASE[a] + b * NQ[a] + j
                    sp.wait_ge(lo_done, PBASE[a] + b * PCH[a] + 2 * j + 2)
                    for blk, part in enumerate((Q_PART, K_PART)[w]):
                        if a == 1 and w == 1:
                            dst = k_stacks_b[b * GPB:(b + 1) * GPB, blk * HD:(blk + 1) * HD, :]
                        else:
                            stacks = ((q_stacks, k_stacks), (q_stacks_b, None))[a][w]
                            g0 = b * GPB + m * (P // HD // GH)
                            dst = stacks[g0:g0 + P // HD // GH, :, blk * HD:(blk + 1) * HD, :]
                        sp.dma_start(dst, parts[0:rows, n % 2, part, :]).then_inc(stacks_stored, 16)

            def load_stack(a, g, buf, q, keys, done):
                for par in range(2):
                    lo = PAR * par
                    qs = (q_stacks, q_stacks_b)[a]
                    sp.dma_start(q[lo:lo + ROWS, buf, par::2, :],
                                 qs[g, par::2].rearrange("a r t -> r a t")).then_inc(done, 16)
                    if a == 0:
                        sp.dma_start(keys[lo:lo + ROWS, buf, :, :],
                                     k_stacks[g, par::2].rearrange("a r t -> r a t")).then_inc(done, 16)
                    else:
                        sp.dma_start(keys[lo:lo + ROWS, buf, 0, :], k_stacks_b[g]).then_inc(done, 16)

            def load_max_stack(a, g, buf):
                if not isinstance(g, int) or g >= 2 or a:
                    sp.wait_ge(max_ready, CHUNKS * (GROUPS * a + g - 1))
                load_stack(a, g, buf, q_max, k_max, max_loaded[buf])

            def load_st_stack(a, g, buf):
                if not isinstance(g, int) or g >= 2 or a:
                    sp.wait_ge(st_ready, GH * UNITS * (GROUPS * a + g - 1))
                load_stack(a, g, buf, q_st, k_st, st_loaded[buf])

            def move_max(a, g, buf, qh):
                n = HALF * (GROUPS * a + g) + qh
                sp.wait_ge(mT_copied, n + 1)
                if not isinstance(g, int) or n >= 4:
                    sp.wait_ge(mrow_loaded, 32 * (n - 3))
                sp.dma_start(max_rows[buf, qh].rearrange("a c (i t) -> (a c i) t", t=P),
                             mT[:, qh, :]).then_inc(mrow_stored, 16)
                sp.wait_ge(mrow_stored, 16 * (n + 1))
                for par in range(2):
                    lo = PAR * par + MROW
                    sp.dma_start(q_st[lo:lo + PARTS, buf, par::2, qh * BANK:(qh + 1) * BANK],
                                 max_rows[buf, qh, par].rearrange("c (i t) -> c i t", i=GH // 2)
                                 ).then_inc(mrow_loaded, 16)

            def store_ctx(a, g, qh):
                sp.wait_ge(ctx_copied, HALF * (GROUPS * a + g) + qh + 1)
                sp.dma_start(ctx_rows[a][g, :, :, qh * BANK:(qh + 1) * BANK], ctx_sb[:, qh, :]).then_inc(ctx_stored, 16)

            def group(a, g, buf, first=False, ahead=2):
                if ahead >= 2:
                    load_max_stack(a, g + 2, buf)
                if ahead >= 1:
                    load_st_stack(a, g + 1, 1 - buf)
                if not first:
                    store_ctx(a, g - 1, 1)
                move_max(a, g, buf, 1)
                store_ctx(a, g, 0)
                if ahead >= 1:
                    move_max(a, g + 1, 1 - buf, 0)

            for a in range(2):
                store_stacks(a, 0)
                sp.wait_ge(stacks_stored, SD * (QBASE[a] + NQ[a]))
                sp.wait_ge(area_set, 5 + a)
                load_max_stack(a, 0, 0)
                load_st_stack(a, 0, 0)
                load_max_stack(a, 1, 1)
                store_stacks(a, 1)
                sp.wait_ge(stacks_stored, SD * (QBASE[a] + BATCH * NQ[a]))
                move_max(a, 0, 0, 0)
                group(a, 0, 0, first=True)
                with sp.Fori(0, (GROUPS - 4) // 2) as i:
                    group(a, 2 * i + 1, 1)
                    group(a, 2 * i + 2, 0)
                group(a, GROUPS - 3, 1)
                group(a, GROUPS - 2, 0, ahead=1)
                group(a, GROUPS - 1, 1, ahead=0)
                store_ctx(a, GROUPS - 1, 1)
                sp.wait_ge(ctx_stored, 16 * HALF * GROUPS * (a + 1))
                for b in range(BATCH):
                    sp.dma_start(sums[:, b, :],
                                 ctx_rows[a][b * GPB:(b + 1) * GPB, :, HD, :].rearrange(
                                     "g i (s c) -> g i s c", c=2 * P)).then_inc(sums_loaded, 16)
                for b in range(BATCH):
                    sp.wait_ge(isums_ready, BATCH * a + b + 1)
                    sp.dma_start(inv_rows[a][b].rearrange("h (s c) -> h s c", c=2 * P),
                                 isums[:, b, :]).then_inc(inv_stored, 16)
                for c in range(BATCH * HALF):
                    b, qh = divmod(c, HALF)
                    if c == 0:
                        sp.wait_ge(inv_stored, 16 * BATCH * (a + 1))
                    if c >= 2:
                        sp.wait_ge(o_ready, 8 * a + 2 * (c - 1))
                    for m in range(DK):
                        g0 = b * GPB + m * (GPB // DK)
                        sp.dma_start(ctxn[:, c % 2, m, :],
                                     ctx_rows[a][g0:g0 + GPB // DK, :, 0:HD, qh * BANK:(qh + 1) * BANK]
                                     ).then_inc(ctx_loaded[c % 2], 16)
                        hs = HEADS // DK
                        sp.dma_start(inv[:, c % 2, m, :],
                                     inv_rows[a][b, m * hs:(m + 1) * hs, qh * BANK:(qh + 1) * BANK].rearrange(
                                         "h (o t) -> h o t", o=1).to_broadcast((hs, HD, BANK))
                                     ).then_inc(ctx_loaded[c % 2], 16)
            for c in range(TILES // 2):
                sp.wait_ge(x_updated, 8 * 3 + c + 1)
                b, t = divmod(2 * c, BT)
                sp.dma_start(out[b, t * P:(t + 2) * P, :].rearrange("(t p) d -> p t d", p=P),
                             x[:, 2 * c:2 * c + 2, :]).then_inc(out_stored, 16)
            sp.wait_ge(out_stored, 16 * (TILES // 2))

        @block.tensor
        def _(pe):
            def norm_transpose(k, b):
                n = 2 * k + b
                for tp in range(BT // 2):
                    pe.wait_ge(ln_xn, BT * n + 2 * tp + 2)
                    if 4 * n + tp >= 2:
                        pe.wait_ge(ln_evac, 4 * n + tp - 1)
                    for t in range(2):
                        for d in range(DK):
                            mm = pe.transpose(psum[:, 6 + tp % 2, (t * DK + d) * P:(t * DK + d + 1) * P],
                                              xn[:, 2 * tp + t, d * P:(d + 1) * P], ident[:])
                    mm.then_inc(ln_tr, 1)

            def project(a, b):
                pe.wait_ge(w_loaded[a], 64)
                pe.wait_ge(ln_evac, 4 * (4 * a + b) + 4)
                for j, (w, m, rows) in enumerate(QUARTERS[a]):
                    for half in range(HALF):
                        n = PBASE[a] + b * PCH[a] + 2 * j + half
                        if n >= 4:
                            pe.wait_ge(rest_done, n - 3)
                        for k in range(DK):
                            mm = pe.matmul(psum[0:rows, n % 4, :], w_a[a][w][:, k, m * P:m * P + rows],
                                           xnT[:, k, b * SEQ + half * BANK:b * SEQ + (half + 1) * BANK],
                                           start=(k == 0), stop=(k == DK - 1))
                        mm.then_inc(proj_ready, 1)
                width = (D, KV_HEADS * HD)[a]
                per = BANK // width
                for v in range(VCH[a]):
                    n = VBASE[a] + b * VCH[a] + v
                    if n >= 2:
                        pe.wait_ge(v_done, n - 1)
                    for t in range(per):
                        tok = b * SEQ + (v * per + t) * P
                        for k in range(DK):
                            mm = pe.matmul(psum[:, 4 + n % 2, t * width:(t + 1) * width], xnT[:, k, tok:tok + P],
                                           w_a[a][2][:, k, :], start=(k == 0), stop=(k == DK - 1))
                    mm.then_inc(v_ready, 1)

            def max_scores(a, g, buf, c):
                qh, r = divmod(c, CPH)
                head, qt = divmod(r, BT // HALF)
                tile, n = qh * (BT // HALF) + qt, CHUNKS * (GROUPS * a + g) + c
                if c == 0:
                    pe.wait_ge(max_loaded[buf], loads(GROUPS * a + g, buf))
                if not isinstance(g, int) or n >= 2:
                    pe.wait_ge(max_used, n - 1)
                q = q_max[:, buf, head, tile * P:(tile + 1) * P]
                keys = k_max[:, buf, 0 if a else head // 2, :]
                slot = psum[:, 2 + 2 * (c % 2):4 + 2 * (c % 2), :].rearrange("p b c -> p (b c)")
                if a == 0:
                    pieces = [(0, 0, BANK), (BANK, BANK, BANK)]
                else:
                    pieces, at = [], 0
                    while at < SEQ:
                        key = ((tile - 1) * P + at) % SEQ
                        size = min(BANK - at % BANK, SEQ - key)
                        pieces.append((at, key, size))
                        at += size
                for at, key, size in pieces:
                    mm = pe.matmul(slot[:, at:at + size], q, keys[:, key:key + size], start=True, stop=True,
                                   skip_group_check=True)
                mm.then_inc(max_ready, 1)

            def turn_max(a, g, qh):
                n = HALF * (GROUPS * a + g) + qh
                pe.wait_ge(mparts_ready, n + 1)
                if not isinstance(g, int) or n >= 1:
                    pe.wait_ge(mT_copied, n)
                pe.sem_inc(turn_started, 1)
                pe.transpose(T_BANK[0:CPH * PARTS, 0:P], mparts[:, qh].rearrange("p a c i -> p (a c i)"),
                             ident_bf[:]).then_inc(mT_ready, 1)

            def scores(a, g, buf, u, head):
                qh, kt = divmod(u, BT)
                n = GH * (UNITS * (GROUPS * a + g) + u) + head
                if head == 0 and u == 0:
                    pe.wait_ge(st_loaded[buf], loads(GROUPS * a + g, buf))
                if head == 0 and kt == 0:
                    pe.wait_ge(mrow_loaded, 32 * (HALF * (GROUPS * a + g) + qh + 1))
                if not isinstance(g, int) or n >= 2:
                    pe.wait_ge(exp_done, n - 1)
                pe.matmul(psum[:, head % 2, :],
                          k_st[:, buf, 0 if a else head // 2, kt * P:(kt + 1) * P],
                          q_st[:, buf, head, qh * BANK:(qh + 1) * BANK],
                          start=True, stop=True).then_inc(st_ready, 1)

            def times_v(a, g, buf, u):
                qh, kt = divmod(u, BT)
                if a == 1 and u in MASKED_UNITS:
                    pe.wait_ge(masked, MPG * g + MASKED_UNITS.index(u) + 1)
                else:
                    pe.wait_ge(exp_done, GH * (UNITS * (GROUPS * a + g) + u + 1))
                if u == 0:
                    pe.wait_ge(vaug_ready, GROUPS * a + g + 1)
                if kt == 0 and (not isinstance(g, int) or HALF * (GROUPS * a + g) + qh > 0):
                    pe.wait_ge(ctx_copied, HALF * (GROUPS * a + g) + qh)
                for head in range(GH):
                    mm = pe.matmul(psum[head * VW:(head + 1) * VW, PV_BANK, :], vaug[:, buf, kt, head, :],
                                   probs[:, u % PRING, head, :], start=(kt == 0), stop=(kt == BT - 1))
                mm.then_inc(pv_done, 1)

            def group(a, g, buf, first=False, ahead=True):
                for u in range(UNITS):
                    if u == 3:
                        turn_max(a, g, 1)
                    if u == 11 and ahead:
                        turn_max(a, g + 1, 0)
                    scores(a, g, buf, u, 0)
                    scores(a, g, buf, u, 1)
                    if ahead:
                        max_scores(a, g + 1, 1 - buf, 2 * u)
                    scores(a, g, buf, u, 2)
                    if ahead:
                        max_scores(a, g + 1, 1 - buf, 2 * u + 1)
                    scores(a, g, buf, u, 3)
                    if u:
                        times_v(a, g, buf, u - 1)
                    elif not first:
                        times_v(a, g - 1, 1 - buf, UNITS - 1)

            def project_out(a):
                for c in range(BATCH * HALF):
                    pe.wait_ge(ctxn_ready, 4 * a + c + 1)
                    for pair in range(2):
                        n = 8 * a + 2 * c + pair
                        if n % 8 >= 2:
                            pe.wait_ge(x_updated, 16 * a + n % 8 - 1)
                        for t in range(2):
                            tok = (2 * pair + t) * P
                            for m in range(DK):
                                mm = pe.matmul(psum[:, pair, t * D:(t + 1) * D], ctxn[:, c % 2, m, tok:tok + P],
                                               w_a[a][3][:, m, :], start=(m == 0), stop=(m == DK - 1))
                        mm.then_inc(o_ready, 1)

            def gate_up(f, c, h):
                for r in range(4):
                    n = 32 * f + 8 * c + 4 * h + r
                    cols = slice(h * 4 * P + r, (h + 1) * 4 * P, 4)
                    for w, base, done in ((wg, 0, gate_ready), (wu, 2, up_ready)):
                        if n >= 2:
                            pe.wait_ge(hid_done, n - 1)
                        for k in range(DK):
                            mm = pe.matmul(psum[:, base + r % 2, :], w[:, k, cols],
                                           xnT[:, k, c * BANK:(c + 1) * BANK], start=(k == 0), stop=(k == DK - 1))
                        mm.then_inc(done, 1)

            def down(f, c):
                pe.wait_ge(sparse_done, 8 * f + 2 * c + 2)
                for pair in range(2):
                    if c:
                        pe.wait_ge(x_updated, 8 * (2 * f + 1) + 2 * (c - 1) + pair + 1)
                    for t in range(2):
                        tok = (2 * pair + t) * P
                        for i in range(INNER // P):
                            mm = pe.matmul(psum[:, 4 + pair, t * D:(t + 1) * D], hid[:, c % 2, i, tok:tok + P],
                                           wd[:, i, :], start=(i == 0), stop=(i == INNER // P - 1))
                    mm.then_inc(down_ready, 1)

            pe.wait_ge(const_ready, 1)
            for a in range(2):
                for b in range(BATCH):
                    norm_transpose(2 * a, b)
                for b in range(BATCH):
                    project(a, b)
                pe.wait_ge(rest_done, PBASE[a] + BATCH * PCH[a])
                pe.wait_ge(v_done, VBASE[a] + BATCH * VCH[a])
                for c in range(CHUNKS):
                    max_scores(a, 0, 0, c)
                    if c == CPH + 6:
                        turn_max(a, 0, 0)
                group(a, 0, 0, first=True)
                with pe.Fori(0, (GROUPS - 2) // 2) as i:
                    group(a, 2 * i + 1, 1)
                    group(a, 2 * i + 2, 0)
                group(a, GROUPS - 1, 1, ahead=False)
                times_v(a, GROUPS - 1, 1, UNITS - 1)
                project_out(a)
                for b in range(BATCH):
                    norm_transpose(2 * a + 1, b)
                if a == 0:
                    pe.wait_ge(wf_loaded, 48)
                for c in range(TOKENS // BANK):
                    if c % HALF == 0:
                        pe.wait_ge(ln_evac, 4 * (2 * (2 * a + 1) + c // HALF) + 4)
                    gate_up(a, c, 0)
                    if c:
                        down(a, c - 1)
                    gate_up(a, c, 1)
                down(a, TOKENS // BANK - 1)

        @block.scalar
        def _(act):
            def norm(k, b):
                n = 2 * k + b
                act.wait_ge(ln_mv, n + 1)
                if n == 0:
                    act.wait_ge(const_ready, 1)
                act.activation(std[:], mv[:, :, 1], ACT.Sqrt, bias=eps[:]).then_inc(ln_sd, 1)

            def copy_transposed(k, b):
                n = 2 * k + b
                for tp in range(BT // 2):
                    act.wait_ge(ln_tr, 4 * n + tp + 1)
                    act.copy(xnT[:, :, (b * BT + 2 * tp) * P:(b * BT + 2 * tp + 2) * P].rearrange(
                        "p d (t c) -> p d t c", t=2),
                        psum[:, 6 + tp % 2, :].rearrange("p (t d c) -> p d t c", t=2, d=DK)).then_inc(ln_evac, 1)

            def split(a):
                total = BATCH * PCH[a]
                for i in range(total + 1):
                    if i < total:
                        b, r = divmod(i, PCH[a])
                        j, half = divmod(r, HALF)
                        w, m, rows = QUARTERS[a][j]
                        n, s = PBASE[a] + i, QBASE[a] + b * NQ[a] + j
                        if s >= 2 and half == 0:
                            act.wait_ge(stacks_stored, SD * (s - 1))
                        act.wait_ge(proj_ready, n + 1)
                        dst = parts[0:rows, s % 2, 0, half * BANK:(half + 1) * BANK]
                        if a == 0:
                            act.activation(dst, psum[0:rows, n % 4, :], ACT.Identity,
                                           bias=bqk[:, w, m:m + 1]).then_inc(hi_done, 1)
                        else:
                            act.copy(dst, psum[0:rows, n % 4, :]).then_inc(hi_done, 1)
                    if i:
                        b, r = divmod(i - 1, PCH[a])
                        j, half = divmod(r, HALF)
                        w, m, rows = QUARTERS[a][j]
                        n, s = PBASE[a] + i - 1, QBASE[a] + b * NQ[a] + j
                        act.wait_ge(rest_done, n + 1)
                        act.copy(parts[0:rows, s % 2, 1, half * BANK:(half + 1) * BANK],
                                 resid[0:rows, n % 2, :]).then_inc(mid_done, 1)

            def exps(a, g, u):
                G = GROUPS * a + g
                if not isinstance(g, int) or UNITS * G + u >= PRING:
                    act.wait_ge(pv_done, UNITS * G + u - PRING + 1)
                for head in range(GH):
                    act.wait_ge(st_ready, GH * (UNITS * G + u) + head + 1)
                    act.activation(probs[:, u % PRING, head, :], psum[:, head % 2, :], ACT.Exp,
                                   scale=SCALE).then_inc(exp_done, 1)

            def copy_ctx(a, g, qh):
                n = HALF * (GROUPS * a + g) + qh
                act.wait_ge(pv_done, UNITS * (GROUPS * a + g) + (qh + 1) * BT)
                if not isinstance(g, int) or n >= 2:
                    act.wait_ge(ctx_stored, 16 * (n - 1))
                act.copy(ctx_sb[:, qh, :], psum[:, PV_BANK, :]).then_inc(ctx_copied, 1)

            def group(a, g, first=False):
                for u in range(UNITS):
                    exps(a, g, u)
                    if u == 0 and not first:
                        copy_ctx(a, g - 1, 1)
                    if u == BT:
                        copy_ctx(a, g, 0)

            def feed_forward(f):
                for c in range(TOKENS // BANK):
                    for h in range(2):
                        for r in range(5):
                            n = 32 * f + 8 * c + 4 * h + r
                            if r < 4:
                                act.wait_ge(gate_ready, n + 1)
                                if n >= 2:
                                    act.wait_ge(hid_done, n - 1)
                                act.activation(gated[:, r % 2, :], psum[:, r % 2, :], ACT.Silu).then_inc(silu_done, 1)
                            if r:
                                act.wait_ge(hid_done, n)
                                if r == 1 and 8 * f + 2 * c + h:
                                    act.wait_ge(wins_done, 3 * (8 * f + 2 * c + h))
                                act.activation(mag[:, r - 1, :], hid[:, c % 2, 4 * h + r - 1, :],
                                               ACT.Abs).then_inc(mag_done, 1)

            act.wait_ge(bias_loaded, 64)
            for a in range(2):
                for b in range(BATCH):
                    norm(2 * a, b)
                    copy_transposed(2 * a, b)
                split(a)
                group(a, 0, first=True)
                with act.Fori(0, (GROUPS - 2) // 2) as i:
                    group(a, 2 * i + 1)
                    group(a, 2 * i + 2)
                group(a, GROUPS - 1)
                copy_ctx(a, GROUPS - 1, 1)
                for b in range(BATCH):
                    norm(2 * a + 1, b)
                    copy_transposed(2 * a + 1, b)
                feed_forward(a)

        @block.vector
        def _(dve):
            def norm(k, b):
                n = 2 * k + b
                if k == 0:
                    dve.wait_ge(x_loaded[b], 16)
                else:
                    dve.wait_ge(x_updated, 8 * (k - 1) + 4 * (b + 1))
                if n:
                    dve.wait_ge(ln_xn, BT * n)
                for t in range(BT):
                    ins = dve.bn_stats(stats[:, t, :], x[:, b * BT + t, :])
                ins.then_inc(ln_stats, 1)
                dve.wait_ge(ln_stats, n + 1)
                for t in range(BT):
                    ins = dve.bn_aggr(mv[:, t, :], stats[:, t, :])
                ins.then_inc(ln_mv, 1)
                dve.wait_ge(ln_sd, n + 1)
                dve.reciprocal(rstd[:], std[:]).then_inc(ln_rstd, 1)
                dve.wait_ge(ln_rstd, n + 1)
                for t in range(BT):
                    if n and t % 2 == 0:
                        dve.wait_ge(ln_tr, 4 * (n - 1) + t // 2 + 1)
                    dve.tensor_scalar(xn[:, t, :], x[:, b * BT + t, :], mv[:, t, 0:1], rstd[:, t:t + 1],
                                      ALU.subtract, ALU.mult).then_inc(ln_xn, 1)

            def copy_v(a, b):
                for v in range(VCH[a]):
                    n = VBASE[a] + b * VCH[a] + v
                    dve.wait_ge(v_ready, n + 1)
                    bank = psum[:, 4 + n % 2, :]
                    if a == 0:
                        dve.tensor_tensor(
                            vsb[:, b * GPB:(b + 1) * GPB, 2 * v:2 * v + 2, :].rearrange("p g k c -> p k g c"),
                            bank.rearrange("p (k g c) -> p k g c", k=2, g=GPB),
                            bv_rows[:].rearrange("p (o g c) -> p o g c", o=1, g=GPB).to_broadcast((P, 2, GPB, GH * HD)),
                            ALU.add).then_inc(v_done, 1)
                    else:
                        dve.tensor_copy(
                            vsb[:, b * GPB:(b + 1) * GPB, :, 0:HD].rearrange("p g k c -> p k g c"),
                            bank.rearrange("p (k g c) -> p k g c", k=BT, g=GPB)).then_inc(v_done, 1)

            def split(a):
                total = BATCH * PCH[a]
                for i in range(total + 1):
                    if i and i % PCH[a] == 0:
                        copy_v(a, i // PCH[a] - 1)
                    if i < total:
                        b, r = divmod(i, PCH[a])
                        j, half = divmod(r, HALF)
                        w, m, rows = QUARTERS[a][j]
                        n, s = PBASE[a] + i, QBASE[a] + b * NQ[a] + j
                        dve.wait_ge(hi_done, n + 1)
                        hi = parts[0:rows, s % 2, 0, half * BANK:(half + 1) * BANK]
                        if n >= 2:
                            dve.wait_ge(lo_done, n - 1)
                        if a == 0:
                            dve.scalar_tensor_tensor(out=resid[0:rows, n % 2, :], in0=psum[0:rows, n % 4, :],
                                                     scalar=bqk[:, w, m:m + 1], in1=hi, op0=ALU.add,
                                                     op1=ALU.subtract).then_inc(rest_done, 1)
                        else:
                            dve.tensor_tensor(resid[0:rows, n % 2, :], psum[0:rows, n % 4, :], hi,
                                              ALU.subtract).then_inc(rest_done, 1)
                    if i:
                        b, r = divmod(i - 1, PCH[a])
                        j, half = divmod(r, HALF)
                        w, m, rows = QUARTERS[a][j]
                        n, s = PBASE[a] + i - 1, QBASE[a] + b * NQ[a] + j
                        dve.wait_ge(mid_done, n + 1)
                        dve.tensor_tensor(parts[0:rows, s % 2, 2, half * BANK:(half + 1) * BANK],
                                          resid[0:rows, n % 2, :],
                                          parts[0:rows, s % 2, 1, half * BANK:(half + 1) * BANK],
                                          ALU.subtract).then_inc(lo_done, 1)

            def maxima(a, g, c):
                qh, r = divmod(c, CPH)
                head, qt = divmod(r, BT // HALF)
                G = GROUPS * a + g
                col = (head % 2) * (CPH // 2) + (head // 2) * (BT // HALF) + qt
                if r == 0 and (not isinstance(g, int) or G >= 1):
                    dve.wait_ge(mparts_ready, HALF * (G - 1) + qh + 1)
                dve.wait_ge(max_ready, CHUNKS * G + c + 1)
                slot = psum[:, 2 + 2 * (c % 2):4 + 2 * (c % 2), :].rearrange("p b c -> p (b c)")
                if a == 0:
                    dve.tensor_reduce(mneg[:, qh, col:col + 1], slot, AX.X, ALU.max, negate=True).then_inc(max_used, 1)
                else:
                    if not isinstance(g, int) or c >= 2 or g:
                        dve.wait_ge(max_used, CHUNKS * G + c - 1)
                    later = 1 if qh * (BT // HALF) + qt else 0
                    dve.tensor_reduce(mrest[:, qh, col:col + 1], slot[:, 2 * P:SEQ], AX.X, ALU.max, negate=True)
                    dve.tensor_tensor_reduce(band_out[:, c % 2, :], slot[:, 0:2 * P], band[:, later, :], 1.0, -3.0e38,
                                             ALU.add, ALU.max, mband[:, qh, col:col + 1]).then_inc(max_used, 1)
                    if r == CPH - 1:
                        dve.wait_ge(max_used, CHUNKS * G + c + 1)
                        dve.scalar_tensor_tensor(out=mneg[:, qh, :], in0=mband[:, qh, :], scalar=-1.0,
                                                 in1=mrest[:, qh, :], op0=ALU.mult, op1=ALU.min).then_inc(cols_ready, 1)

            def copy_turned(a, g, qh):
                n = HALF * (GROUPS * a + g) + qh
                dve.wait_ge(mT_ready, n + 1)
                if not isinstance(g, int) or n >= 2:
                    dve.wait_ge(mrow_stored, 16 * (n - 1))
                dve.tensor_copy(mT[:, qh, :], T_BANK[0:CPH * PARTS, 0:P]).then_inc(mT_copied, 1)

            def group(a, g, ahead=True):
                for u in range(UNITS):
                    if ahead:
                        maxima(a, g + 1, 2 * u)
                        maxima(a, g + 1, 2 * u + 1)
                    if u == 3:
                        copy_turned(a, g, 1)
                    if u == 11 and ahead:
                        copy_turned(a, g + 1, 0)

            def project_out(a):
                for b in range(BATCH):
                    dve.wait_ge(sums_loaded, 16 * BATCH * (a + 1))
                    dve.reciprocal(isums[:, b, :], sums[:, b, :]).then_inc(isums_ready, 1)
                if a == 0:
                    dve.wait_ge(x_biased, 1)
                for c in range(BATCH * HALF):
                    dve.wait_ge(ctx_loaded[c % 2], 64 * (2 * a + c // 2 + 1))
                    dve.tensor_tensor(ctxn[:, c % 2], ctxn[:, c % 2], inv[:, c % 2], ALU.mult).then_inc(ctxn_ready, 1)
                    for pair in range(2):
                        n = 2 * c + pair
                        dve.wait_ge(o_ready, 8 * a + n + 1)
                        xs = x[:, 2 * n:2 * n + 2, :].rearrange("p t d -> p (t d)")
                        dve.tensor_tensor(xs, psum[:, pair, :], xs, ALU.add).then_inc(x_updated, 1)

            def feed_forward(f):
                for c in range(TOKENS // BANK):
                    for h in range(2):
                        n0 = 8 * f + 2 * c + h
                        if c >= 2 and h == 0:
                            dve.wait_ge(down_ready, 8 * f + 2 * (c - 1))
                        for r in range(4):
                            n = 4 * n0 + r
                            dve.wait_ge(up_ready, n + 1)
                            dve.wait_ge(silu_done, n + 1)
                            dve.tensor_tensor(hid[:, c % 2, 4 * h + r, :], psum[:, 2 + r % 2, :], gated[:, r % 2, :],
                                              ALU.mult).then_inc(hid_done, 1)
                        if h == 0 and c:
                            add_down(f, c - 1)
                        dve.wait_ge(mag_done, 4 * (n0 + 1))
                        if n0:
                            dve.wait_ge(tally2_done, 4 * n0)
                        for lo, w0, w1 in ((0, 0, 3), (1, 3, 5), (2, 5, 6)):
                            k = w1 - w0
                            dve.tensor_tensor(wins[:, w0:w1, :], mag[:, lo:lo + 1, :].to_broadcast((P, k, BANK)),
                                              mag[:, lo + 1:4, :], ALU.is_ge).then_inc(wins_done, 1)
                        dve.wait_ge(wins_done, 3 * (n0 + 1))
                        if n0:
                            dve.wait_ge(sparse_done, n0)
                        for r, (i, j, op) in enumerate(((0, 1, ALU.add), (3, 4, ALU.add), (5, 1, ALU.subtract),
                                                        (2, 4, ALU.add))):
                            dve.tensor_tensor(tally[:, r, :], wins[:, i, :], wins[:, j, :], op).then_inc(tally_done, 1)
                        for r, (i, op) in enumerate(((2, ALU.add), (0, ALU.subtract), (3, ALU.subtract), (5, ALU.add))):
                            dve.wait_ge(tally_done, 4 * n0 + r + 1)
                            dve.tensor_tensor(tally2[:, r, :], tally[:, r, :], wins[:, i, :], op).then_inc(tally2_done, 1)
                        for r, (need, op) in enumerate(((2.0, ALU.is_ge), (1.0, ALU.is_ge), (0.0, ALU.is_ge),
                                                        (1.0, ALU.is_le))):
                            dve.wait_ge(tally2_done, 4 * n0 + r + 1)
                            ins = dve.scalar_tensor_tensor(out=hid[:, c % 2, 4 * h + r, :], in0=tally2[:, r, :], scalar=need,
                                                           in1=hid[:, c % 2, 4 * h + r, :], op0=op, op1=ALU.mult)
                        ins.then_inc(sparse_done, 1)
                add_down(f, TOKENS // BANK - 1)

            def add_down(f, c):
                for pair in range(2):
                    dve.wait_ge(down_ready, 8 * f + 2 * c + pair + 1)
                    xs = x[:, 4 * c + 2 * pair:4 * c + 2 * pair + 2, :].rearrange("p t d -> p (t d)")
                    dve.tensor_tensor(xs, psum[:, 4 + pair, :], xs, ALU.add).then_inc(x_updated, 1)

            dve.wait_ge(bias_loaded, 64)
            for a in range(2):
                for b in range(BATCH):
                    norm(2 * a, b)
                split(a)
                for c in range(CHUNKS):
                    maxima(a, 0, c)
                    if c == CPH + 7:
                        copy_turned(a, 0, 0)
                group(a, 0)
                with dve.Fori(0, (GROUPS - 2) // 2) as i:
                    group(a, 2 * i + 1)
                    group(a, 2 * i + 2)
                group(a, GROUPS - 1, ahead=False)
                project_out(a)
                for b in range(BATCH):
                    norm(2 * a + 1, b)
                feed_forward(a)

        @block.gpsimd
        def _(pool):
            pool.memset(ident[:], 0.0).then_inc(area_set, 1)
            pool.wait_ge(area_set, 1)
            pool.affine_select(out=ident[:], in_=ident[:], compare_op=ALU.not_equal, fill=1.0, base=0,
                               pattern=[[-1, P]], channel_multiplier=1).then_inc(split_done, 1)
            pool.wait_ge(split_done, 1)
            pool.tensor_copy(ident_bf[:], ident[:])
            pool.memset(nought[:], 0.0)
            pool.memset(eps[:], EPS).then_inc(const_ready, 1)

            def set_area():
                for t, value in ((q_max, 0.0), (q_st, 0.0), (k_max, 1.0), (k_st, 1.0)):
                    pool.memset(t, value)
                pool.memset(vaug[:].rearrange("p a b c d -> p (a b c d)"), 1.0).then_inc(area_set, 1)

            def extend_v(a, g, buf):
                G = GROUPS * a + g
                if not isinstance(g, int) or g >= 2:
                    pool.wait_ge(pv_done, UNITS * (G - 1))
                if isinstance(g, int) and g == 0:
                    pool.wait_ge(v_done, VBASE[a] + BATCH * VCH[a])
                pool.wait_ge(area_set, 5 + a)
                src = vsb[:, g, :, 0:(GH * HD, HD)[a]]
                if a == 0:
                    src = src.rearrange("p k (h d) -> p k h d", d=HD)
                else:
                    src = src.rearrange("p k (h d) -> p k h d", h=1).to_broadcast((P, BT, GH, HD))
                pool.tensor_copy(vaug[:, buf, :, :, 0:HD], src).then_inc(vaug_ready, 1)

            def split_max(a, g, qh):
                G = GROUPS * a + g
                n = HALF * G + qh
                if a == 0:
                    pool.wait_ge(max_used, CHUNKS * G + CPH * (qh + 1))
                else:
                    pool.wait_ge(cols_ready, HALF * g + qh + 1)
                if not isinstance(g, int) or n >= 2:
                    pool.wait_ge(mT_ready, n - 1)

                def view(t):
                    return t[:, qh, :].rearrange("p (a i) -> p a i", a=2)

                s0 = 1 + 4 * n
                pool.tensor_tensor(mparts[:, qh, :, 0, :], view(mneg), view(nought), ALU.add).then_inc(split_done, 1)
                pool.wait_ge(split_done, s0 + 1)
                pool.tensor_tensor(view(mres1), view(mneg), mparts[:, qh, :, 0, :], ALU.subtract).then_inc(split_done, 1)
                pool.wait_ge(split_done, s0 + 2)
                pool.tensor_tensor(mparts[:, qh, :, 1, :], view(mres1), view(nought), ALU.add).then_inc(split_done, 1)
                pool.wait_ge(split_done, s0 + 3)
                pool.tensor_tensor(view(mres2), view(mres1), mparts[:, qh, :, 1, :], ALU.subtract).then_inc(split_done, 1)
                pool.wait_ge(split_done, s0 + 4)
                pool.tensor_tensor(mparts[:, qh, :, 2, :], view(mres2), view(nought), ALU.add).then_inc(mparts_ready, 1)

            def mask_probs(a, g, u):
                pool.wait_ge(exp_done, GH * (UNITS * (GROUPS * a + g) + u + 1))
                pool.sem_inc(mask_started, 1)
                for kind, tile in masked_blocks(u):
                    v = probs[:, u % PRING, :, tile * P:(tile + 1) * P]
                    if kind == 0:
                        ins = pool.affine_select(out=v, in_=v, compare_op=ALU.is_ge, fill=0.0, base=0,
                                                 pattern=[[0, GH], [-1, P]], channel_multiplier=1)
                    else:
                        ins = pool.affine_select(out=v, in_=v, compare_op=ALU.is_gt, fill=0.0, base=0,
                                                 pattern=[[0, GH], [1, P]], channel_multiplier=-1)
                ins.then_inc(masked, 1)

            def group(a, g, buf, ahead=True):
                for u in range(UNITS):
                    if a == 1 and u in MASKED_UNITS:
                        mask_probs(a, g, u)
                    if u == 1:
                        split_max(a, g, 1)
                    if u == 4 and ahead:
                        extend_v(a, g + 1, 1 - buf)
                    if u == 9 and ahead:
                        split_max(a, g + 1, 0)

            pool.memset(band[:], MASK).then_inc(area_set, 1)
            pool.wait_ge(area_set, 2)
            pool.affine_select(out=band[:], in_=band[:], compare_op=ALU.is_ge, fill=0.0, base=0,
                               pattern=[[0, 2], [1, 2 * P]], channel_multiplier=-1).then_inc(area_set, 1)
            pool.wait_ge(area_set, 3)
            pool.affine_select(out=band[:], in_=band[:], compare_op=ALU.is_gt, fill=0.0, base=WINDOW,
                               pattern=[[0, 2], [-1, 2 * P]], channel_multiplier=1).then_inc(area_set, 1)
            pool.wait_ge(area_set, 4)
            pool.memset(band[:, 0, 0:P], 0.0)
            for a in range(2):
                if a == 1:
                    pool.wait_ge(down_ready, 8)
                set_area()
                if a == 0:
                    pool.wait_ge(bias_loaded, 64)
                    pool.wait_ge(ln_xn, BATCH * BT)
                    pool.tensor_tensor(x[:], x[:], bo_rows[:].rearrange("p (o d) -> p o d", o=1).to_broadcast(
                        (P, TILES, D)), ALU.add).then_inc(x_biased, 1)
                pool.wait_ge(area_set, 5 + a)
                extend_v(a, 0, 0)
                split_max(a, 0, 0)
                group(a, 0, 0)
                with pool.Fori(0, (GROUPS - 2) // 2) as i:
                    group(a, 2 * i + 1, 1)
                    group(a, 2 * i + 2, 0)
                group(a, GROUPS - 1, 1, ahead=False)


_INS = ["L0_attn_a_hidden_states", "L0_attn_a_Wq", "L0_attn_a_bq", "L0_attn_a_Wk", "L0_attn_a_bk", "L0_attn_a_Wv",
        "L0_attn_a_bv", "L0_attn_a_Wo", "L0_attn_a_bo", "L0_attn_b_wq", "L0_attn_b_wk", "L0_attn_b_wv",
        "L0_attn_b_wo", "L0_ffn_w_gate", "L0_ffn_w_up", "L0_ffn_w_down"]
_OUTS = [((2, 1024, 256), "float32")]


def kernel(**inputs):
    import numpy as _np
    import concourse.bacc as _bacc
    from concourse import mybir as _mybir
    from concourse.bass_utils import run_bass_kernel_spmd as _run

    nc = _bacc.Bacc("TRN2", target_bir_lowering=False, num_devices=1)
    arrays, args = {}, []
    for name in _INS:
        a = _np.ascontiguousarray(inputs[name])
        arrays[f"in_{name}_dram"] = a
        args.append(nc.dram_tensor(f"in_{name}_dram", a.shape, _mybir.dt.from_np(a.dtype), kind="ExternalInput").ap())
    for i, (shape, dtype) in enumerate(_OUTS):
        dt = _mybir.dt.from_np(_np.dtype(dtype))
        args.append(nc.dram_tensor(f"out_{i}_dram", shape, dt, kind="ExternalOutput").ap())
    hybrid_kernel(nc, *args)
    r = _run(nc, [arrays], core_ids=[0])
    return r.results[0]["out_0_dram"]
```

```python
from contextlib import ExitStack

import concourse.bass as bass
from concourse import mybir

F32 = mybir.dt.float32
BF16 = mybir.dt.bfloat16
ALU = mybir.AluOpType
ACT = mybir.ActivationFunctionType
AX = mybir.AxisListType

P = 128
BATCH, SEQ, D = 2, 1024, 256
TOKENS = BATCH * SEQ
TILES = TOKENS // P
BT = SEQ // P
DK = D // P
HEADS, HD = 32, 8
KV_HEADS = 8
WINDOW = 128
MASK = -10000000000.0
SCALE = 1.0 / float(HD) ** 0.5
EPS = 1e-5
INNER = 1024
BANK = 512
HALF = SEQ // BANK

GH = 4
GPB = HEADS // GH
GROUPS = BATCH * GPB
PARTS = 3
Q_PART = (0, 0, 1, 1, 0, 2)
K_PART = (0, 1, 0, 1, 2, 0)
ROWS = HD * len(Q_PART)
MROW = ROWS + 8
PAR = 64
UNITS = HALF * BT
CHUNKS = GH * BT
CPH = CHUNKS // HALF
PRING = 4
AREA = 23552
TWO_ONES = 1.0019378662109375
VW = 32


def masked_blocks(unit):
    qh, kt = divmod(unit, BT)
    return [(kind, kt + kind - qh * (BANK // P)) for kind in (0, 1)
            if kt + kind < BT and (kt + kind) // (BANK // P) == qh]


MASKED_UNITS = [u for u in range(UNITS) if masked_blocks(u)]
MPG = len(MASKED_UNITS)


def hybrid_kernel(nc, x_in, wq_a, bq_a, wk_a, bk_a, wv_a, bv_a, wo_a, bo_a,
                  wq_b, wk_b, wv_b, wo_b, w_gate, w_up, w_down, out):
    ctx = ExitStack()
    with ctx:
        def sb(name, shape, dt=F32):
            return ctx.enter_context(nc.sbuf_tensor(name, shape, dt))

        def sem(name):
            return ctx.enter_context(nc.semaphore(name))

        def dram(name, shape, dt):
            return nc.dram_tensor(name, shape, dt, kind="Internal").ap()

        q_stacks = dram("q_stacks", (GROUPS, GH, ROWS, SEQ), BF16)
        k_stacks = dram("k_stacks", (GROUPS, GH, ROWS, SEQ), BF16)
        k_stacks_b = dram("k_stacks_b", (GROUPS, ROWS, SEQ), BF16)
        q_stacks_b = dram("q_stacks_b", (GROUPS, GH, ROWS, SEQ), BF16)
        max_rows = dram("max_rows", (2, HALF, 2, PARTS, GH // 2 * BANK), BF16)
        ctx_rows = [dram(f"ctx_rows{a}", (GROUPS, GH, VW, SEQ), F32) for a in range(2)]
        inv_rows = [dram(f"inv_rows{a}", (BATCH, HEADS, SEQ), F32) for a in range(2)]

        x = sb("x", [P, TILES, D])
        xn = sb("xn", [P, BT, D])
        xnT = sb("xnT", [P, DK, TOKENS])
        stats = sb("stats", [P, BT, 6])
        mv = sb("mv", [P, BT, 2])
        std = sb("std", [P, BT])
        rstd = sb("rstd", [P, BT])
        eps = sb("eps", [P, 1])
        ident = sb("ident", [P, P])
        ident_bf = sb("ident_bf", [P, P], BF16)
        wqkvo = [sb(f"wqkvo{i}", [P, DK, D]) for i in range(4)]
        wqo_b = [sb(f"wqo_b{i}", [P, DK, D]) for i in range(2)]
        wkv_b = [sb(f"wkv_b{i}", [P, DK, KV_HEADS * HD]) for i in range(2)]
        wg = sb("wg", [P, DK, INNER])
        wu = sb("wu", [P, DK, INNER])
        wd = sb("wd", [P, INNER // P, D])
        bqk = sb("bqk", [P, 2, DK])
        bv_rows = sb("bv_rows", [P, D])
        bo_rows = sb("bo_rows", [P, D])
        band = sb("band", [P, 2, 2 * P])
        band_out = sb("band_out", [P, 2, 2 * P])
        vsb = sb("vsb", [P, GROUPS, BT, GH * HD])
        mneg = sb("mneg", [P, HALF, CPH])
        mband = sb("mband", [P, HALF, CPH])
        mrest = sb("mrest", [P, HALF, CPH])
        mres1 = sb("mres1", [P, HALF, CPH])
        mres2 = sb("mres2", [P, HALF, CPH])
        nought = sb("nought", [P, HALF, CPH])
        mparts = sb("mparts", [P, HALF, 2, PARTS, CPH // 2], BF16)
        mT = sb("mT", [CPH * PARTS, HALF, P], BF16)
        sums = sb("sums", [P, BATCH, 2 * P])
        isums = sb("isums", [P, BATCH, 2 * P])
        area = sb("area", [P, AREA])

        def carve(at, shape, dt):
            n = 1
            for size in shape:
                n *= size
            end = at + n * (4 if dt == F32 else 2) // 4
            assert end <= AREA, end
            v = area[:, at:end]
            if dt != F32:
                v = v.bitcast(dt)
            names = "abcd"[:len(shape)]
            return v.rearrange("p (" + " ".join(names) + ") -> p " + " ".join(names),
                               **dict(zip(names, shape))), end

        probs, at = carve(0, [PRING, GH, BANK], F32)
        ctx_sb, at = carve(at, [HALF, BANK], F32)
        ones_at = at
        k_max, at = carve(at, [2, GH // 2, SEQ], BF16)
        k_st, at = carve(at, [2, GH // 2, SEQ], BF16)
        vaug_at = at
        vaug, at = carve(at, [2, BT, GH, VW], F32)
        q_st_at = at
        q_st, at = carve(at, [2, GH, SEQ], BF16)
        q_max_at = at
        q_max, at = carve(at, [2, GH, SEQ], BF16)
        q_max_end = at
        hid, at = carve(0, [2, INNER // P, BANK], F32)
        gated, at = carve(at, [2, BANK], F32)
        mag, at = carve(at, [4, BANK], F32)
        wins, at = carve(at, [6, BANK], BF16)
        tally, at = carve(at, [4, BANK], BF16)
        tally2, at = carve(at, [4, BANK], BF16)
        assert at <= q_st_at
        parts, at = carve(q_st_at, [2, PARTS, SEQ], BF16)
        resid, at = carve(at, [2, BANK], F32)
        assert at <= q_max_at
        ctxn, at = carve(q_max_at, [2, DK, BANK], F32)
        inv, at = carve(at, [2, DK, BANK], F32)
        assert at <= q_max_end

        psum = ctx.enter_context(nc.psum_tensor("psum", [P, 8, BANK], F32))
        T_BANK = psum[:, 7, :].bitcast(BF16)
        PV_BANK = 6

        x_loaded = [sem(f"x_loaded{b}") for b in range(BATCH)]
        w_loaded = [sem("wa_loaded"), sem("wb_loaded")]
        wf_loaded = sem("wf_loaded")
        bias_loaded = sem("bias_loaded")
        stacks_stored = [sem(f"stacks_stored{i}") for i in range(2)]
        max_loaded = [sem(f"max_stack_loaded{i}") for i in range(2)]
        st_loaded = [sem(f"stack_loaded{i}") for i in range(2)]
        mrow_stored = sem("mrow_stored")
        mrow_loaded = sem("mrow_loaded")
        ctx_stored = sem("ctx_stored")
        sums_loaded = sem("sums_loaded")
        inv_stored = sem("inv_stored")
        ctx_loaded = [sem(f"ctx_loaded{i}") for i in range(2)]
        out_stored = sem("out_stored")
        const_ready = sem("const_ready")
        area_set = sem("area_set")
        ln_stats, ln_mv, ln_sd, ln_rstd, ln_xn = (sem(s) for s in ("ln_stats", "ln_mv", "ln_sd", "ln_rstd", "ln_xn"))
        ln_tr, ln_evac = sem("ln_tr"), sem("ln_evac")
        proj_ready, hi_done, rest_done, mid_done, lo_done = (
            sem(s) for s in ("proj_ready", "hi_done", "rest_done", "mid_done", "lo_done"))
        v_ready, v_done = sem("v_ready"), sem("v_done")
        vaug_ready = sem("vaug_ready")
        max_ready, max_used = sem("max_ready"), sem("max_used")
        cols_ready, split_done, mparts_ready = sem("cols_ready"), sem("split_done"), sem("mparts_ready")
        mT_ready, mT_copied = sem("mT_ready"), sem("mT_copied")
        st_ready, exp_done, masked, pv_done, ctx_copied = (
            sem(s) for s in ("st_ready", "exp_done", "masked", "pv_done", "ctx_copied"))
        isums_ready, ctxn_ready, o_ready = sem("isums_ready"), sem("ctxn_ready"), sem("o_ready")
        turn_started, mask_started = sem("turn_started"), sem("mask_started")
        x_biased, x_attended, x_fed = sem("x_biased"), sem("x_attended"), sem("x_fed")
        gate_ready, up_ready, silu_done, hid_done, mag_done, wins_done, tally_done, tally2_done, sparse_done, down_ready = (
            sem(s) for s in ("gate_ready", "up_ready", "silu_done", "hid_done", "mag_done", "wins_done",
                             "tally_done", "tally2_done", "sparse_done", "down_ready"))

        QUARTERS = [
            [(0, 0, P), (0, 1, P), (1, 0, P), (1, 1, P)],
            [(0, 0, P), (0, 1, P), (1, 0, KV_HEADS * HD)],
        ]
        PCH = [2 * len(q) for q in QUARTERS]
        PBASE = [0, BATCH * PCH[0]]
        VCH = [BT // 2, 1]
        VBASE = [0, BATCH * VCH[0]]
        SD = 16 * len(Q_PART)
        NQ = [len(q) for q in QUARTERS]
        QBASE = [0, BATCH * NQ[0]]
        w_a = [[wqkvo[0], wqkvo[1], wqkvo[2], wqkvo[3]], [wqo_b[0], wkv_b[0], wkv_b[1], wqo_b[1]]]
        STACK_DMAS = 64

        def stored(slot, pairs):
            return SD * ((pairs + 1 - slot) // 2)

        def loads(G, buf):
            return STACK_DMAS // 2 * (G - buf) + STACK_DMAS

        block = ctx.enter_context(nc.Block())

        @block.sync
        def _(sp):
            for b in range(BATCH):
                sp.dma_start(x[:, b * BT:(b + 1) * BT, :],
                             x_in[b].rearrange("(t p) d -> p t d", p=P)).then_inc(x_loaded[b], 16)
            for w, src in zip(wqkvo, (wq_a, wk_a, wv_a, wo_a)):
                sp.dma_start(w[:], src.rearrange("(k p) n -> p k n", p=P)).then_inc(w_loaded[0], 16)
            for i, src in enumerate((bq_a, bk_a)):
                sp.dma_start(bqk[:, i, :], src.rearrange("(m p) -> p m", p=P),
                             allow_slow_non_contiguous=True).then_inc(bias_loaded, 16)
            for dst, src in ((bv_rows, bv_a), (bo_rows, bo_a)):
                sp.dma_start(dst[:], src.rearrange("(o d) -> o d", o=1).to_broadcast((P, D))).then_inc(bias_loaded, 16)
            for w, src in zip((*wqo_b, *wkv_b), (wq_b, wo_b, wk_b, wv_b)):
                sp.dma_start(w[:], src.rearrange("(k p) n -> p k n", p=P)).then_inc(w_loaded[1], 16)
            for w, src in ((wg, w_gate), (wu, w_up)):
                sp.dma_start(w[:], src.rearrange("(k p) n -> p k n", p=P)).then_inc(wf_loaded, 16)
            sp.dma_start(wd[:].rearrange("p (h r) n -> p h r n", h=2),
                         w_down.rearrange("(h p r) n -> p h r n", h=2, r=4)).then_inc(wf_loaded, 16)

            def store_stacks(a, b):
                for j, (w, m, rows) in enumerate(QUARTERS[a]):
                    n = QBASE[a] + b * NQ[a] + j
                    sp.wait_ge(lo_done, PBASE[a] + b * PCH[a] + 2 * j + 2)
                    for blk, part in enumerate((Q_PART, K_PART)[w]):
                        if a == 1 and w == 1:
                            dst = k_stacks_b[b * GPB:(b + 1) * GPB, blk * HD:(blk + 1) * HD, :]
                        else:
                            stacks = ((q_stacks, k_stacks), (q_stacks_b, None))[a][w]
                            g0 = b * GPB + m * (P // HD // GH)
                            dst = stacks[g0:g0 + P // HD // GH, :, blk * HD:(blk + 1) * HD, :]
                        sp.dma_start(dst, parts[0:rows, n % 2, part, :]).then_inc(stacks_stored[n % 2], 16)

            def load_stack(a, g, buf, q, keys, done):
                for par in range(2):
                    lo = PAR * par
                    qs = (q_stacks, q_stacks_b)[a]
                    sp.dma_start(q[lo:lo + ROWS, buf, par::2, :],
                                 qs[g, par::2].rearrange("a r t -> r a t")).then_inc(done, 16)
                    if a == 0:
                        sp.dma_start(keys[lo:lo + ROWS, buf, :, :],
                                     k_stacks[g, par::2].rearrange("a r t -> r a t")).then_inc(done, 16)
                    else:
                        sp.dma_start(keys[lo:lo + ROWS, buf, 0, :], k_stacks_b[g]).then_inc(done, 16)

            def load_max_stack(a, g, buf):
                if not isinstance(g, int) or g >= 2 or a:
                    sp.wait_ge(max_ready, CHUNKS * (GROUPS * a + g - 1))
                load_stack(a, g, buf, q_max, k_max, max_loaded[buf])

            def load_st_stack(a, g, buf):
                if not isinstance(g, int) or g >= 2 or a:
                    sp.wait_ge(st_ready, GH * UNITS * (GROUPS * a + g - 1))
                load_stack(a, g, buf, q_st, k_st, st_loaded[buf])

            def move_max(a, g, buf, qh):
                n = HALF * (GROUPS * a + g) + qh
                sp.wait_ge(mT_copied, n + 1)
                if not isinstance(g, int) or n >= 4:
                    sp.wait_ge(mrow_loaded, 32 * (n - 3))
                sp.dma_start(max_rows[buf, qh].rearrange("a c (i t) -> (a c i) t", t=P),
                             mT[:, qh, :]).then_inc(mrow_stored, 16)
                sp.wait_ge(mrow_stored, 16 * (n + 1))
                for par in range(2):
                    lo = PAR * par + MROW
                    sp.dma_start(q_st[lo:lo + PARTS, buf, par::2, qh * BANK:(qh + 1) * BANK],
                                 max_rows[buf, qh, par].rearrange("c (i t) -> c i t", i=GH // 2)
                                 ).then_inc(mrow_loaded, 16)

            def store_ctx(a, g, qh):
                sp.wait_ge(ctx_copied, HALF * (GROUPS * a + g) + qh + 1)
                sp.dma_start(ctx_rows[a][g, :, :, qh * BANK:(qh + 1) * BANK], ctx_sb[:, qh, :]).then_inc(ctx_stored, 16)

            def group(a, g, buf, first=False, ahead=2):
                if ahead >= 2:
                    load_max_stack(a, g + 2, buf)
                if ahead >= 1:
                    load_st_stack(a, g + 1, 1 - buf)
                if not first:
                    store_ctx(a, g - 1, 1)
                move_max(a, g, buf, 1)
                store_ctx(a, g, 0)
                if ahead >= 1:
                    move_max(a, g + 1, 1 - buf, 0)

            def store_inverses(a, b):
                sp.dma_start(sums[:, b, :],
                             ctx_rows[a][b * GPB:(b + 1) * GPB, :, HD, :].rearrange(
                                 "g i (s c) -> g i s c", c=2 * P)).then_inc(sums_loaded, 16)
                sp.wait_ge(isums_ready, BATCH * a + b + 1)
                sp.dma_start(inv_rows[a][b].rearrange("h (s c) -> h s c", c=2 * P),
                             isums[:, b, :]).then_inc(inv_stored, 16)
                sp.wait_ge(inv_stored, 16 * (BATCH * a + b + 1))

            def load_ctx(a, b):
                for c in (HALF * b, HALF * b + 1):
                    qh = c % HALF
                    if c >= 2:
                        sp.wait_ge(o_ready, 8 * a + 2 * (c - 1))
                    for m in range(DK):
                        g0 = b * GPB + m * (GPB // DK)
                        hs = HEADS // DK
                        sp.dma_start(ctxn[:, c % 2, m, :],
                                     ctx_rows[a][g0:g0 + GPB // DK, :, 0:HD, qh * BANK:(qh + 1) * BANK]
                                     ).then_inc(ctx_loaded[c % 2], 16)
                        sp.dma_start(inv[:, c % 2, m, :],
                                     inv_rows[a][b, m * hs:(m + 1) * hs, qh * BANK:(qh + 1) * BANK].rearrange(
                                         "h (o t) -> h o t", o=1).to_broadcast((hs, HD, BANK))
                                     ).then_inc(ctx_loaded[c % 2], 16)

            for a in range(2):
                store_stacks(a, 0)
                for i in range(2):
                    sp.wait_ge(stacks_stored[i], stored(i, QBASE[a] + NQ[a]))
                sp.wait_ge(area_set, 5 + 2 * a)
                load_max_stack(a, 0, 0)
                load_max_stack(a, 1, 1)
                store_stacks(a, 1)
                for i in range(2):
                    sp.wait_ge(stacks_stored[i], stored(i, QBASE[a] + BATCH * NQ[a]))
                sp.wait_ge(area_set, 6 + 2 * a)
                load_st_stack(a, 0, 0)
                move_max(a, 0, 0, 0)
                group(a, 0, 0, first=True)
                with sp.Fori(0, GPB // 2) as i:
                    group(a, 2 * i + 1, 1)
                    group(a, 2 * i + 2, 0)
                sp.wait_ge(ctx_stored, 16 * (HALF * (GROUPS * a + GPB) + 1))
                store_inverses(a, 0)
                with sp.Fori(GPB // 2, (GROUPS - 4) // 2) as i:
                    group(a, 2 * i + 1, 1)
                    group(a, 2 * i + 2, 0)
                group(a, GROUPS - 3, 1)
                group(a, GROUPS - 2, 0, ahead=1)
                sp.wait_ge(max_ready, CHUNKS * GROUPS * (a + 1))
                load_ctx(a, 0)
                group(a, GROUPS - 1, 1, ahead=0)
                store_ctx(a, GROUPS - 1, 1)
                sp.wait_ge(ctx_stored, 16 * HALF * GROUPS * (a + 1))
                store_inverses(a, 1)
                load_ctx(a, 1)
            for c in range(TILES // 2):
                sp.wait_ge(x_fed, 8 + c + 1)
                b, t = divmod(2 * c, BT)
                sp.dma_start(out[b, t * P:(t + 2) * P, :].rearrange("(t p) d -> p t d", p=P),
                             x[:, 2 * c:2 * c + 2, :]).then_inc(out_stored, 16)
            sp.wait_ge(out_stored, 16 * (TILES // 2))

        @block.tensor
        def _(pe):
            def norm_transpose(k, b):
                n = 2 * k + b
                for tp in range(BT // 2):
                    pe.wait_ge(ln_xn, BT * n + 2 * tp + 2)
                    if 4 * n + tp >= 2:
                        pe.wait_ge(ln_evac, 4 * n + tp - 1)
                    for t in range(2):
                        for d in range(DK):
                            mm = pe.transpose(psum[:, 6 + tp % 2, (t * DK + d) * P:(t * DK + d + 1) * P],
                                              xn[:, 2 * tp + t, d * P:(d + 1) * P], ident[:])
                    mm.then_inc(ln_tr, 1)

            def project(a, b):
                pe.wait_ge(w_loaded[a], 64)
                pe.wait_ge(ln_evac, 4 * (4 * a + b) + 4)
                if a == 1:
                    pe.wait_ge(hid_done, 8 * (3, 4)[b])
                for j, (w, m, rows) in enumerate(QUARTERS[a]):
                    for half in range(HALF):
                        n = PBASE[a] + b * PCH[a] + 2 * j + half
                        if n >= 4:
                            pe.wait_ge(rest_done, n - 3)
                        for k in range(DK):
                            mm = pe.matmul(psum[0:rows, n % 4, :], w_a[a][w][:, k, m * P:m * P + rows],
                                           xnT[:, k, b * SEQ + half * BANK:b * SEQ + (half + 1) * BANK],
                                           start=(k == 0), stop=(k == DK - 1))
                        mm.then_inc(proj_ready, 1)
                width = (D, KV_HEADS * HD)[a]
                per = BANK // width
                for v in range(VCH[a]):
                    n = VBASE[a] + b * VCH[a] + v
                    if n >= 2:
                        pe.wait_ge(v_done, n - 1)
                    for t in range(per):
                        tok = b * SEQ + (v * per + t) * P
                        for k in range(DK):
                            mm = pe.matmul(psum[:, 4 + n % 2, t * width:(t + 1) * width], xnT[:, k, tok:tok + P],
                                           w_a[a][2][:, k, :], start=(k == 0), stop=(k == DK - 1))
                    mm.then_inc(v_ready, 1)

            def max_scores(a, g, buf, c, split=False):
                qh, r = divmod(c, CPH)
                head, qt = divmod(r, BT // HALF)
                tile, n = qh * (BT // HALF) + qt, CHUNKS * (GROUPS * a + g) + c
                if c == 0:
                    pe.wait_ge(max_loaded[buf], loads(GROUPS * a + g, buf))
                if not isinstance(g, int) or n >= 2:
                    pe.wait_ge(max_used, n - 1)
                q = q_max[:, buf, head, tile * P:(tile + 1) * P]
                keys = k_max[:, buf, 0 if a else head // 2, :]
                slot = psum[:, 2 + 2 * (c % 2):4 + 2 * (c % 2), :].rearrange("p b c -> p (b c)")
                if a == 0:
                    pieces = [(0, 0, BANK), (BANK, BANK, BANK)]
                else:
                    pieces, at = [], 0
                    while at < SEQ:
                        key = ((tile - 1) * P + at) % SEQ
                        size = min(BANK - at % BANK, SEQ - key)
                        pieces.append((at, key, size))
                        at += size

                def multiply(some):
                    for at, key, size in some:
                        mm = pe.matmul(slot[:, at:at + size], q, keys[:, key:key + size], start=True, stop=True,
                                       skip_group_check=True)
                    return mm

                def rest():
                    multiply([p for p in pieces if p[0] >= BANK]).then_inc(max_ready, 1)

                multiply([p for p in pieces if p[0] < BANK])
                if split:
                    return rest
                rest()

            def turn_max(a, g, qh):
                n = HALF * (GROUPS * a + g) + qh
                pe.wait_ge(mparts_ready, n + 1)
                if not isinstance(g, int) or n >= 1:
                    pe.wait_ge(mT_copied, n)
                pe.sem_inc(turn_started, 1)
                pe.transpose(T_BANK[0:CPH * PARTS, 0:P], mparts[:, qh].rearrange("p a c i -> p (a c i)"),
                             ident_bf[:]).then_inc(mT_ready, 1)

            def scores(a, g, buf, u, head):
                qh, kt = divmod(u, BT)
                n = GH * (UNITS * (GROUPS * a + g) + u) + head
                if head == 0 and u == 0:
                    pe.wait_ge(st_loaded[buf], loads(GROUPS * a + g, buf))
                if head == 0 and kt == 0:
                    pe.wait_ge(mrow_loaded, 32 * (HALF * (GROUPS * a + g) + qh + 1))
                if not isinstance(g, int) or n >= 2:
                    pe.wait_ge(exp_done, n - 1)
                pe.matmul(psum[:, head % 2, :],
                          k_st[:, buf, 0 if a else head // 2, kt * P:(kt + 1) * P],
                          q_st[:, buf, head, qh * BANK:(qh + 1) * BANK],
                          start=True, stop=True).then_inc(st_ready, 1)

            def times_v(a, g, buf, u):
                qh, kt = divmod(u, BT)
                if a == 1 and u in MASKED_UNITS:
                    pe.wait_ge(masked, MPG * g + MASKED_UNITS.index(u) + 1)
                else:
                    pe.wait_ge(exp_done, GH * (UNITS * (GROUPS * a + g) + u + 1))
                if u == 0:
                    pe.wait_ge(vaug_ready, GROUPS * a + g + 1)
                if kt == 0 and (not isinstance(g, int) or HALF * (GROUPS * a + g) + qh > 0):
                    pe.wait_ge(ctx_copied, HALF * (GROUPS * a + g) + qh)
                for head in range(GH):
                    mm = pe.matmul(psum[head * VW:(head + 1) * VW, PV_BANK, :], vaug[:, buf, kt, head, :],
                                   probs[:, u % PRING, head, :], start=(kt == 0), stop=(kt == BT - 1))
                mm.then_inc(pv_done, 1)

            def group(a, g, buf, first=False, ahead=True):
                for u in range(UNITS):
                    if u == 3:
                        turn_max(a, g, 1)
                    if u == 11 and ahead:
                        turn_max(a, g + 1, 0)
                    scores(a, g, buf, u, 0)
                    scores(a, g, buf, u, 1)
                    if ahead:
                        max_scores(a, g + 1, 1 - buf, 2 * u)
                        second = max_scores(a, g + 1, 1 - buf, 2 * u + 1, split=True)
                    scores(a, g, buf, u, 2)
                    if ahead:
                        second()
                    scores(a, g, buf, u, 3)
                    if u:
                        times_v(a, g, buf, u - 1)
                    elif not first:
                        times_v(a, g - 1, 1 - buf, UNITS - 1)

            def project_out(a, b):
                if b == 0:
                    pe.wait_ge(ctx_copied, HALF * GROUPS * (a + 1))
                for c in (HALF * b, HALF * b + 1):
                    pe.wait_ge(ctxn_ready, 4 * a + c + 1)
                    for pair in range(2):
                        n = 2 * (c % HALF) + pair
                        if n >= 2:
                            pe.wait_ge(x_attended, 8 * a + 4 * b + n - 1)
                        for t in range(2):
                            tok = (2 * pair + t) * P
                            for m in range(DK):
                                mm = pe.matmul(psum[:, 6 + pair, t * D:(t + 1) * D], ctxn[:, c % 2, m, tok:tok + P],
                                               w_a[a][3][:, m, :], start=(m == 0), stop=(m == DK - 1))
                        mm.then_inc(o_ready, 1)

            def gate_up(f, c, h):
                pe.wait_ge(ln_evac, 4 * (2 * (2 * f + 1) + c // HALF) + 4)
                if f == 0 and c == 3 and h == 0:
                    pe.wait_ge(rest_done, PBASE[1] + PCH[1])
                for r in range(4):
                    n = 32 * f + 8 * c + 4 * h + r
                    cols = slice(h * 4 * P + r, (h + 1) * 4 * P, 4)
                    for w, base, done in ((wg, 0, gate_ready), (wu, 2, up_ready)):
                        if n >= 2:
                            pe.wait_ge(hid_done, n - 1)
                        for k in range(DK):
                            mm = pe.matmul(psum[:, base + r % 2, :], w[:, k, cols],
                                           xnT[:, k, c * BANK:(c + 1) * BANK], start=(k == 0), stop=(k == DK - 1))
                        mm.then_inc(done, 1)

            def down(f, c):
                pe.wait_ge(sparse_done, 8 * f + 2 * c + 2)
                for pair in range(2):
                    if c:
                        pe.wait_ge(x_fed, 8 * f + 2 * (c - 1) + pair + 1)
                    if f == 0 and c == 2:
                        pe.wait_ge(v_done, VBASE[1] + VCH[1])
                    for t in range(2):
                        tok = (2 * pair + t) * P
                        for i in range(INNER // P):
                            mm = pe.matmul(psum[:, 4 + pair, t * D:(t + 1) * D], hid[:, c % 2, i, tok:tok + P],
                                           wd[:, i, :], start=(i == 0), stop=(i == INNER // P - 1))
                    mm.then_inc(down_ready, 1)

            def attend(a):
                pe.wait_ge(rest_done, PBASE[a] + BATCH * PCH[a])
                pe.wait_ge(v_done, VBASE[a] + BATCH * VCH[a])
                for c in range(CHUNKS):
                    max_scores(a, 0, 0, c)
                    if c == CPH + 6:
                        turn_max(a, 0, 0)
                group(a, 0, 0, first=True)
                with pe.Fori(0, (GROUPS - 2) // 2) as i:
                    group(a, 2 * i + 1, 1)
                    group(a, 2 * i + 2, 0)
                group(a, GROUPS - 1, 1, ahead=False)
                times_v(a, GROUPS - 1, 1, UNITS - 1)

            pe.wait_ge(const_ready, 1)
            for b in range(BATCH):
                norm_transpose(0, b)
            for b in range(BATCH):
                project(0, b)
            for a in range(2):
                attend(a)
                project_out(a, 0)
                norm_transpose(2 * a + 1, 0)
                if a == 0:
                    pe.wait_ge(wf_loaded, 48)
                gate_up(a, 0, 0)
                gate_up(a, 0, 1)
                project_out(a, 1)
                gate_up(a, 1, 0)
                down(a, 0)
                norm_transpose(2 * a + 1, 1)
                gate_up(a, 1, 1)
                gate_up(a, 2, 0)
                down(a, 1)
                gate_up(a, 2, 1)
                if a == 0:
                    norm_transpose(2, 0)
                    project(1, 0)
                gate_up(a, 3, 0)
                down(a, 2)
                gate_up(a, 3, 1)
                down(a, 3)
                if a == 0:
                    norm_transpose(2, 1)
                    project(1, 1)

        @block.scalar
        def _(act):
            def norm(k, b):
                n = 2 * k + b
                act.wait_ge(ln_mv, n + 1)
                if n == 0:
                    act.wait_ge(const_ready, 1)
                act.activation(std[:], mv[:, :, 1], ACT.Sqrt, bias=eps[:]).then_inc(ln_sd, 1)

            def copy_transposed(k, b):
                n = 2 * k + b
                for tp in range(BT // 2):
                    act.wait_ge(ln_tr, 4 * n + tp + 1)
                    act.copy(xnT[:, :, (b * BT + 2 * tp) * P:(b * BT + 2 * tp + 2) * P].rearrange(
                        "p d (t c) -> p d t c", t=2),
                        psum[:, 6 + tp % 2, :].rearrange("p (t d c) -> p d t c", t=2, d=DK)).then_inc(ln_evac, 1)

            def split(a, b):
                for i in range(PCH[a] + 1):
                    if i < PCH[a]:
                        j, half = divmod(i, HALF)
                        w, m, rows = QUARTERS[a][j]
                        n, s = PBASE[a] + b * PCH[a] + i, QBASE[a] + b * NQ[a] + j
                        if s >= 2 and half == 0:
                            act.wait_ge(stacks_stored[s % 2], stored(s % 2, s - 1))
                        act.wait_ge(proj_ready, n + 1)
                        dst = parts[0:rows, s % 2, 0, half * BANK:(half + 1) * BANK]
                        if a == 0:
                            act.activation(dst, psum[0:rows, n % 4, :], ACT.Identity,
                                           bias=bqk[:, w, m:m + 1]).then_inc(hi_done, 1)
                        else:
                            act.copy(dst, psum[0:rows, n % 4, :]).then_inc(hi_done, 1)
                    if i:
                        j, half = divmod(i - 1, HALF)
                        w, m, rows = QUARTERS[a][j]
                        n, s = PBASE[a] + b * PCH[a] + i - 1, QBASE[a] + b * NQ[a] + j
                        act.wait_ge(rest_done, n + 1)
                        act.copy(parts[0:rows, s % 2, 1, half * BANK:(half + 1) * BANK],
                                 resid[0:rows, n % 2, :]).then_inc(mid_done, 1)

            def exps(a, g, u):
                G = GROUPS * a + g
                if not isinstance(g, int) or UNITS * G + u >= PRING:
                    act.wait_ge(pv_done, UNITS * G + u - PRING + 1)
                for head in range(GH):
                    act.wait_ge(st_ready, GH * (UNITS * G + u) + head + 1)
                    act.activation(probs[:, u % PRING, head, :], psum[:, head % 2, :], ACT.Exp,
                                   scale=SCALE).then_inc(exp_done, 1)

            def copy_ctx(a, g, qh):
                n = HALF * (GROUPS * a + g) + qh
                act.wait_ge(pv_done, UNITS * (GROUPS * a + g) + (qh + 1) * BT)
                if not isinstance(g, int) or n >= 2:
                    act.wait_ge(ctx_stored, 16 * (n - 1))
                act.copy(ctx_sb[:, qh, :], psum[:, PV_BANK, :]).then_inc(ctx_copied, 1)

            def group(a, g, first=False):
                for u in range(UNITS):
                    exps(a, g, u)
                    if u == 0 and not first:
                        copy_ctx(a, g - 1, 1)
                    if u == BT:
                        copy_ctx(a, g, 0)

            def silu_and_size(f, c, h):
                if c == 0 and h == 0:
                    act.wait_ge(ctx_stored, 16 * HALF * GROUPS * (f + 1))
                for r in range(5):
                    n = 32 * f + 8 * c + 4 * h + r
                    if r < 4:
                        act.wait_ge(gate_ready, n + 1)
                        if n >= 2:
                            act.wait_ge(hid_done, n - 1)
                        act.activation(gated[:, r % 2, :], psum[:, r % 2, :], ACT.Silu).then_inc(silu_done, 1)
                    if r:
                        act.wait_ge(hid_done, n)
                        if r == 1 and 8 * f + 2 * c + h:
                            act.wait_ge(wins_done, 3 * (8 * f + 2 * c + h))
                        act.activation(mag[:, r - 1, :], hid[:, c % 2, 4 * h + r - 1, :],
                                       ACT.Abs).then_inc(mag_done, 1)

            def attend(a):
                group(a, 0, first=True)
                with act.Fori(0, (GROUPS - 2) // 2) as i:
                    group(a, 2 * i + 1)
                    group(a, 2 * i + 2)
                group(a, GROUPS - 1)
                copy_ctx(a, GROUPS - 1, 1)

            act.wait_ge(bias_loaded, 64)
            for b in range(BATCH):
                norm(0, b)
                copy_transposed(0, b)
            for b in range(BATCH):
                split(0, b)
            for a in range(2):
                attend(a)
                norm(2 * a + 1, 0)
                copy_transposed(2 * a + 1, 0)
                silu_and_size(a, 0, 0)
                silu_and_size(a, 0, 1)
                silu_and_size(a, 1, 0)
                norm(2 * a + 1, 1)
                copy_transposed(2 * a + 1, 1)
                silu_and_size(a, 1, 1)
                silu_and_size(a, 2, 0)
                silu_and_size(a, 2, 1)
                if a == 0:
                    norm(2, 0)
                    copy_transposed(2, 0)
                    split(1, 0)
                silu_and_size(a, 3, 0)
                silu_and_size(a, 3, 1)
                if a == 0:
                    norm(2, 1)
                    copy_transposed(2, 1)
                    split(1, 1)

        @block.vector
        def _(dve):
            def norm(k, b):
                n = 2 * k + b
                if k == 0:
                    dve.wait_ge(x_loaded[b], 16)
                elif k % 2:
                    dve.wait_ge(x_attended, 8 * (k // 2) + 4 * (b + 1))
                else:
                    dve.wait_ge(x_fed, 4 * (b + 1))
                if n:
                    dve.wait_ge(ln_xn, BT * n)
                for t in range(BT):
                    ins = dve.bn_stats(stats[:, t, :], x[:, b * BT + t, :])
                ins.then_inc(ln_stats, 1)
                dve.wait_ge(ln_stats, n + 1)
                for t in range(BT):
                    ins = dve.bn_aggr(mv[:, t, :], stats[:, t, :])
                ins.then_inc(ln_mv, 1)
                dve.wait_ge(ln_sd, n + 1)
                dve.reciprocal(rstd[:], std[:]).then_inc(ln_rstd, 1)
                dve.wait_ge(ln_rstd, n + 1)
                for t in range(BT):
                    if n and t % 2 == 0:
                        dve.wait_ge(ln_tr, 4 * (n - 1) + t // 2 + 1)
                    dve.tensor_scalar(xn[:, t, :], x[:, b * BT + t, :], mv[:, t, 0:1], rstd[:, t:t + 1],
                                      ALU.subtract, ALU.mult).then_inc(ln_xn, 1)

            def copy_v(a, b):
                for v in range(VCH[a]):
                    n = VBASE[a] + b * VCH[a] + v
                    dve.wait_ge(v_ready, n + 1)
                    bank = psum[:, 4 + n % 2, :]
                    if a == 0:
                        dve.tensor_tensor(
                            vsb[:, b * GPB:(b + 1) * GPB, 2 * v:2 * v + 2, :].rearrange("p g k c -> p k g c"),
                            bank.rearrange("p (k g c) -> p k g c", k=2, g=GPB),
                            bv_rows[:].rearrange("p (o g c) -> p o g c", o=1, g=GPB).to_broadcast((P, 2, GPB, GH * HD)),
                            ALU.add).then_inc(v_done, 1)
                    else:
                        dve.tensor_copy(
                            vsb[:, b * GPB:(b + 1) * GPB, :, 0:HD].rearrange("p g k c -> p k g c"),
                            bank.rearrange("p (k g c) -> p k g c", k=BT, g=GPB)).then_inc(v_done, 1)

            def split(a, b):
                for i in range(PCH[a] + 1):
                    if i < PCH[a]:
                        j, half = divmod(i, HALF)
                        w, m, rows = QUARTERS[a][j]
                        n, s = PBASE[a] + b * PCH[a] + i, QBASE[a] + b * NQ[a] + j
                        dve.wait_ge(hi_done, n + 1)
                        hi = parts[0:rows, s % 2, 0, half * BANK:(half + 1) * BANK]
                        if n >= 2:
                            dve.wait_ge(lo_done, n - 1)
                        if a == 0:
                            dve.scalar_tensor_tensor(out=resid[0:rows, n % 2, :], in0=psum[0:rows, n % 4, :],
                                                     scalar=bqk[:, w, m:m + 1], in1=hi, op0=ALU.add,
                                                     op1=ALU.subtract).then_inc(rest_done, 1)
                        else:
                            dve.tensor_tensor(resid[0:rows, n % 2, :], psum[0:rows, n % 4, :], hi,
                                              ALU.subtract).then_inc(rest_done, 1)
                    if i:
                        j, half = divmod(i - 1, HALF)
                        w, m, rows = QUARTERS[a][j]
                        n, s = PBASE[a] + b * PCH[a] + i - 1, QBASE[a] + b * NQ[a] + j
                        dve.wait_ge(mid_done, n + 1)
                        dve.tensor_tensor(parts[0:rows, s % 2, 2, half * BANK:(half + 1) * BANK],
                                          resid[0:rows, n % 2, :],
                                          parts[0:rows, s % 2, 1, half * BANK:(half + 1) * BANK],
                                          ALU.subtract).then_inc(lo_done, 1)
                copy_v(a, b)

            def maxima(a, g, c):
                qh, r = divmod(c, CPH)
                head, qt = divmod(r, BT // HALF)
                G = GROUPS * a + g
                col = (head % 2) * (CPH // 2) + (head // 2) * (BT // HALF) + qt
                if r == 0 and (not isinstance(g, int) or G >= 1):
                    dve.wait_ge(mparts_ready, HALF * (G - 1) + qh + 1)
                dve.wait_ge(max_ready, CHUNKS * G + c + 1)
                slot = psum[:, 2 + 2 * (c % 2):4 + 2 * (c % 2), :].rearrange("p b c -> p (b c)")
                if a == 0:
                    dve.tensor_reduce(mneg[:, qh, col:col + 1], slot, AX.X, ALU.max, negate=True).then_inc(max_used, 1)
                else:
                    if not isinstance(g, int) or c >= 2 or g:
                        dve.wait_ge(max_used, CHUNKS * G + c - 1)
                    later = 1 if qh * (BT // HALF) + qt else 0
                    dve.tensor_reduce(mrest[:, qh, col:col + 1], slot[:, 2 * P:SEQ], AX.X, ALU.max, negate=True)
                    dve.tensor_tensor_reduce(band_out[:, c % 2, :], slot[:, 0:2 * P], band[:, later, :], 1.0, -3.0e38,
                                             ALU.add, ALU.max, mband[:, qh, col:col + 1]).then_inc(max_used, 1)
                    if r == CPH - 1:
                        dve.wait_ge(max_used, CHUNKS * G + c + 1)
                        dve.scalar_tensor_tensor(out=mneg[:, qh, :], in0=mband[:, qh, :], scalar=-1.0,
                                                 in1=mrest[:, qh, :], op0=ALU.mult, op1=ALU.min).then_inc(cols_ready, 1)

            def copy_turned(a, g, qh):
                n = HALF * (GROUPS * a + g) + qh
                dve.wait_ge(mT_ready, n + 1)
                if not isinstance(g, int) or n >= 2:
                    dve.wait_ge(mrow_stored, 16 * (n - 1))
                dve.tensor_copy(mT[:, qh, :], T_BANK[0:CPH * PARTS, 0:P]).then_inc(mT_copied, 1)

            def group(a, g, ahead=True):
                for u in range(UNITS):
                    if ahead:
                        maxima(a, g + 1, 2 * u)
                        maxima(a, g + 1, 2 * u + 1)
                    if u == 3:
                        copy_turned(a, g, 1)
                    if u == 11 and ahead:
                        copy_turned(a, g + 1, 0)

            def invert_sums(a, b):
                dve.wait_ge(sums_loaded, 16 * (BATCH * a + b + 1))
                dve.reciprocal(isums[:, b, :], sums[:, b, :]).then_inc(isums_ready, 1)

            def divide_ctx(a, c):
                dve.wait_ge(ctx_loaded[c % 2], 64 * (2 * a + c // 2 + 1))
                dve.tensor_tensor(ctxn[:, c % 2], ctxn[:, c % 2], inv[:, c % 2], ALU.mult).then_inc(ctxn_ready, 1)

            def add_attention(a, c):
                for pair in range(2):
                    n = 2 * c + pair
                    dve.wait_ge(o_ready, 8 * a + n + 1)
                    xs = x[:, 2 * n:2 * n + 2, :].rearrange("p t d -> p (t d)")
                    dve.tensor_tensor(xs, psum[:, 6 + pair, :], xs, ALU.add).then_inc(x_attended, 1)

            def hidden(f, c, h):
                n0 = 8 * f + 2 * c + h
                if c >= 2 and h == 0:
                    dve.wait_ge(down_ready, 8 * f + 2 * (c - 1))
                for r in range(4):
                    n = 4 * n0 + r
                    dve.wait_ge(up_ready, n + 1)
                    dve.wait_ge(silu_done, n + 1)
                    dve.tensor_tensor(hid[:, c % 2, 4 * h + r, :], psum[:, 2 + r % 2, :], gated[:, r % 2, :],
                                      ALU.mult).then_inc(hid_done, 1)
                if h == 0 and c:
                    add_down(f, c - 1)
                dve.wait_ge(mag_done, 4 * (n0 + 1))
                if n0:
                    dve.wait_ge(tally2_done, 4 * n0)
                for lo, w0, w1 in ((0, 0, 3), (1, 3, 5), (2, 5, 6)):
                    k = w1 - w0
                    dve.tensor_tensor(wins[:, w0:w1, :], mag[:, lo:lo + 1, :].to_broadcast((P, k, BANK)),
                                      mag[:, lo + 1:4, :], ALU.is_ge).then_inc(wins_done, 1)
                dve.wait_ge(wins_done, 3 * (n0 + 1))
                if n0:
                    dve.wait_ge(sparse_done, n0)
                for r, (i, j, op) in enumerate(((0, 1, ALU.add), (3, 4, ALU.add), (5, 1, ALU.subtract),
                                                (2, 4, ALU.add))):
                    dve.tensor_tensor(tally[:, r, :], wins[:, i, :], wins[:, j, :], op).then_inc(tally_done, 1)
                for r, (i, op) in enumerate(((2, ALU.add), (0, ALU.subtract), (3, ALU.subtract), (5, ALU.add))):
                    dve.wait_ge(tally_done, 4 * n0 + r + 1)
                    dve.tensor_tensor(tally2[:, r, :], tally[:, r, :], wins[:, i, :], op).then_inc(tally2_done, 1)
                for r, (need, op) in enumerate(((2.0, ALU.is_ge), (1.0, ALU.is_ge), (0.0, ALU.is_ge),
                                                (1.0, ALU.is_le))):
                    dve.wait_ge(tally2_done, 4 * n0 + r + 1)
                    ins = dve.scalar_tensor_tensor(out=hid[:, c % 2, 4 * h + r, :], in0=tally2[:, r, :], scalar=need,
                                                   in1=hid[:, c % 2, 4 * h + r, :], op0=op, op1=ALU.mult)
                ins.then_inc(sparse_done, 1)

            def add_down(f, c):
                for pair in range(2):
                    dve.wait_ge(down_ready, 8 * f + 2 * c + pair + 1)
                    xs = x[:, 4 * c + 2 * pair:4 * c + 2 * pair + 2, :].rearrange("p t d -> p (t d)")
                    dve.tensor_tensor(xs, psum[:, 4 + pair, :], xs, ALU.add).then_inc(x_fed, 1)

            def attend(a):
                for c in range(CHUNKS):
                    maxima(a, 0, c)
                    if c == CPH + 7:
                        copy_turned(a, 0, 0)
                group(a, 0)
                with dve.Fori(0, GPB // 2) as i:
                    group(a, 2 * i + 1)
                    group(a, 2 * i + 2)
                invert_sums(a, 0)
                with dve.Fori(GPB // 2, (GROUPS - 2) // 2) as i:
                    group(a, 2 * i + 1)
                    group(a, 2 * i + 2)
                group(a, GROUPS - 1, ahead=False)
                divide_ctx(a, 0)
                divide_ctx(a, 1)

            dve.wait_ge(bias_loaded, 64)
            for b in range(BATCH):
                norm(0, b)
            for b in range(BATCH):
                split(0, b)
            for a in range(2):
                attend(a)
                if a == 0:
                    dve.wait_ge(x_biased, 1)
                add_attention(a, 0)
                add_attention(a, 1)
                norm(2 * a + 1, 0)
                invert_sums(a, 1)
                hidden(a, 0, 0)
                hidden(a, 0, 1)
                for c in (2, 3):
                    divide_ctx(a, c)
                    add_attention(a, c)
                hidden(a, 1, 0)
                norm(2 * a + 1, 1)
                hidden(a, 1, 1)
                hidden(a, 2, 0)
                hidden(a, 2, 1)
                if a == 0:
                    norm(2, 0)
                    split(1, 0)
                hidden(a, 3, 0)
                hidden(a, 3, 1)
                add_down(a, 3)
                if a == 0:
                    norm(2, 1)
                    split(1, 1)

        @block.gpsimd
        def _(pool):
            pool.memset(ident[:], 0.0).then_inc(area_set, 1)
            pool.wait_ge(area_set, 1)
            pool.affine_select(out=ident[:], in_=ident[:], compare_op=ALU.not_equal, fill=1.0, base=0,
                               pattern=[[-1, P]], channel_multiplier=1).then_inc(split_done, 1)
            pool.wait_ge(split_done, 1)
            pool.tensor_copy(ident_bf[:], ident[:])
            pool.memset(nought[:], 0.0)
            pool.memset(eps[:], EPS).then_inc(const_ready, 1)

            def set_area(first):
                if first:
                    pool.memset(area[:, q_max_at:q_max_end], 0.0)
                    pool.memset(area[:, ones_at:vaug_at], TWO_ONES)
                    pool.memset(area[:, vaug_at:q_st_at], 1.0).then_inc(area_set, 1)
                else:
                    pool.memset(area[:, q_st_at:q_max_at], 0.0).then_inc(area_set, 1)

            def extend_v(a, g, buf):
                G = GROUPS * a + g
                if not isinstance(g, int) or g >= 2:
                    pool.wait_ge(pv_done, UNITS * (G - 1))
                if isinstance(g, int) and g == 0:
                    pool.wait_ge(v_done, VBASE[a] + BATCH * VCH[a])
                pool.wait_ge(area_set, 5 + 2 * a)
                src = vsb[:, g, :, 0:(GH * HD, HD)[a]]
                if a == 0:
                    src = src.rearrange("p k (h d) -> p k h d", d=HD)
                else:
                    src = src.rearrange("p k (h d) -> p k h d", h=1).to_broadcast((P, BT, GH, HD))
                pool.tensor_copy(vaug[:, buf, :, :, 0:HD], src).then_inc(vaug_ready, 1)

            def split_max(a, g, qh):
                G = GROUPS * a + g
                n = HALF * G + qh
                if a == 0:
                    pool.wait_ge(max_used, CHUNKS * G + CPH * (qh + 1))
                else:
                    pool.wait_ge(cols_ready, HALF * g + qh + 1)
                if not isinstance(g, int) or n >= 2:
                    pool.wait_ge(mT_ready, n - 1)

                def view(t):
                    return t[:, qh, :].rearrange("p (a i) -> p a i", a=2)

                s0 = 1 + 4 * n
                pool.tensor_tensor(mparts[:, qh, :, 0, :], view(mneg), view(nought), ALU.add).then_inc(split_done, 1)
                pool.wait_ge(split_done, s0 + 1)
                pool.tensor_tensor(view(mres1), view(mneg), mparts[:, qh, :, 0, :], ALU.subtract).then_inc(split_done, 1)
                pool.wait_ge(split_done, s0 + 2)
                pool.tensor_tensor(mparts[:, qh, :, 1, :], view(mres1), view(nought), ALU.add).then_inc(split_done, 1)
                pool.wait_ge(split_done, s0 + 3)
                pool.tensor_tensor(view(mres2), view(mres1), mparts[:, qh, :, 1, :], ALU.subtract).then_inc(split_done, 1)
                pool.wait_ge(split_done, s0 + 4)
                pool.tensor_tensor(mparts[:, qh, :, 2, :], view(mres2), view(nought), ALU.add).then_inc(mparts_ready, 1)

            def mask_probs(a, g, u):
                pool.wait_ge(exp_done, GH * (UNITS * (GROUPS * a + g) + u + 1))
                pool.sem_inc(mask_started, 1)
                for kind, tile in masked_blocks(u):
                    v = probs[:, u % PRING, :, tile * P:(tile + 1) * P]
                    if kind == 0:
                        ins = pool.affine_select(out=v, in_=v, compare_op=ALU.is_ge, fill=0.0, base=0,
                                                 pattern=[[0, GH], [-1, P]], channel_multiplier=1)
                    else:
                        ins = pool.affine_select(out=v, in_=v, compare_op=ALU.is_gt, fill=0.0, base=0,
                                                 pattern=[[0, GH], [1, P]], channel_multiplier=-1)
                ins.then_inc(masked, 1)

            def group(a, g, buf, ahead=True):
                for u in range(UNITS):
                    if a == 1 and u in MASKED_UNITS:
                        mask_probs(a, g, u)
                    if u == 1:
                        split_max(a, g, 1)
                    if u == 4 and ahead:
                        extend_v(a, g + 1, 1 - buf)
                    if u == 9 and ahead:
                        split_max(a, g + 1, 0)

            pool.memset(band[:], MASK).then_inc(area_set, 1)
            pool.wait_ge(area_set, 2)
            pool.affine_select(out=band[:], in_=band[:], compare_op=ALU.is_ge, fill=0.0, base=0,
                               pattern=[[0, 2], [1, 2 * P]], channel_multiplier=-1).then_inc(area_set, 1)
            pool.wait_ge(area_set, 3)
            pool.affine_select(out=band[:], in_=band[:], compare_op=ALU.is_gt, fill=0.0, base=WINDOW,
                               pattern=[[0, 2], [-1, 2 * P]], channel_multiplier=1).then_inc(area_set, 1)
            pool.wait_ge(area_set, 4)
            pool.memset(band[:, 0, 0:P], 0.0)
            for a in range(2):
                if a == 1:
                    pool.wait_ge(down_ready, 8)
                set_area(first=True)
                if a == 0:
                    pool.wait_ge(bias_loaded, 64)
                    pool.wait_ge(ln_xn, BATCH * BT)
                    pool.tensor_tensor(x[:], x[:], bo_rows[:].rearrange("p (o d) -> p o d", o=1).to_broadcast(
                        (P, TILES, D)), ALU.add).then_inc(x_biased, 1)
                for i in range(2):
                    pool.wait_ge(stacks_stored[i], stored(i, QBASE[a] + BATCH * NQ[a]))
                set_area(first=False)
                pool.wait_ge(area_set, 5 + 2 * a)
                extend_v(a, 0, 0)
                split_max(a, 0, 0)
                group(a, 0, 0)
                with pool.Fori(0, (GROUPS - 2) // 2) as i:
                    group(a, 2 * i + 1, 1)
                    group(a, 2 * i + 2, 0)
                group(a, GROUPS - 1, 1, ahead=False)


_INS = ["L0_attn_a_hidden_states", "L0_attn_a_Wq", "L0_attn_a_bq", "L0_attn_a_Wk", "L0_attn_a_bk", "L0_attn_a_Wv",
        "L0_attn_a_bv", "L0_attn_a_Wo", "L0_attn_a_bo", "L0_attn_b_wq", "L0_attn_b_wk", "L0_attn_b_wv",
        "L0_attn_b_wo", "L0_ffn_w_gate", "L0_ffn_w_up", "L0_ffn_w_down"]
_OUTS = [((2, 1024, 256), "float32")]


def kernel(**inputs):
    import numpy as _np
    import concourse.bacc as _bacc
    from concourse import mybir as _mybir
    from concourse.bass_utils import run_bass_kernel_spmd as _run

    nc = _bacc.Bacc("TRN2", target_bir_lowering=False, num_devices=1)
    arrays, args = {}, []
    for name in _INS:
        a = _np.ascontiguousarray(inputs[name])
        arrays[f"in_{name}_dram"] = a
        args.append(nc.dram_tensor(f"in_{name}_dram", a.shape, _mybir.dt.from_np(a.dtype), kind="ExternalInput").ap())
    for i, (shape, dtype) in enumerate(_OUTS):
        dt = _mybir.dt.from_np(_np.dtype(dtype))
        args.append(nc.dram_tensor(f"out_{i}_dram", shape, dt, kind="ExternalOutput").ap())
    hybrid_kernel(nc, *args)
    r = _run(nc, [arrays], core_ids=[0])
    return r.results[0]["out_0_dram"]
```

```python
from contextlib import ExitStack

import concourse.bass as bass
from concourse import mybir

F32 = mybir.dt.float32
BF16 = mybir.dt.bfloat16
ALU = mybir.AluOpType
ACT = mybir.ActivationFunctionType
AX = mybir.AxisListType

P = 128
BATCH, SEQ, D = 2, 1024, 256
TOKENS = BATCH * SEQ
TILES = TOKENS // P
BT = SEQ // P
DK = D // P
HEADS, HD = 32, 8
KV_HEADS = 8
WINDOW = 128
MASK = -10000000000.0
SCALE = 1.0 / float(HD) ** 0.5
EPS = 1e-5
INNER = 1024
BANK = 512
HALF = SEQ // BANK

GH = 4
GPB = HEADS // GH
GROUPS = BATCH * GPB
PARTS = 3
BLOCKS = 6
RUNS = ((0, 3), (3, 2), (5, 1))
ROWS = HD * BLOCKS
MROW = ROWS + 8
PAR = 64
UNITS = HALF * BT
CHUNKS = GH * BT
CPH = CHUNKS // HALF
LEAD = 24
PRING = 4
AREA = 23552
TWO_ONES = 1.0019378662109375
VW = 32


def masked_blocks(unit):
    qh, kt = divmod(unit, BT)
    return [(kind, kt + kind - qh * (BANK // P)) for kind in (0, 1)
            if kt + kind < BT and (kt + kind) // (BANK // P) == qh]


MASKED_UNITS = [u for u in range(UNITS) if masked_blocks(u)]
MPG = len(MASKED_UNITS)


def hybrid_kernel(nc, x_in, wq_a, bq_a, wk_a, bk_a, wv_a, bv_a, wo_a, bo_a,
                  wq_b, wk_b, wv_b, wo_b, w_gate, w_up, w_down, out):
    ctx = ExitStack()
    with ctx:
        def sb(name, shape, dt=F32):
            return ctx.enter_context(nc.sbuf_tensor(name, shape, dt))

        def sem(name):
            return ctx.enter_context(nc.semaphore(name))

        def dram(name, shape, dt):
            return nc.dram_tensor(name, shape, dt, kind="Internal").ap()

        q_stacks = dram("q_stacks", (GROUPS, GH, HD, BLOCKS, SEQ), BF16)
        k_stacks = dram("k_stacks", (GROUPS, GH, HD, BLOCKS, SEQ), BF16)
        k_stacks_b = dram("k_stacks_b", (GROUPS, HD, BLOCKS, SEQ), BF16)
        q_stacks_b = dram("q_stacks_b", (GROUPS, GH, HD, BLOCKS, SEQ), BF16)
        max_rows = dram("max_rows", (2, HALF, 2, PARTS, GH // 2 * BANK), BF16)
        ctx_rows = [dram(f"ctx_rows{a}", (GROUPS, GH, VW, SEQ), F32) for a in range(2)]
        inv_rows = [dram(f"inv_rows{a}", (BATCH, HEADS, SEQ), F32) for a in range(2)]

        x = sb("x", [P, TILES, D])
        xn = sb("xn", [P, BT, D])
        xnT = sb("xnT", [P, DK, TOKENS])
        stats = sb("stats", [P, BT, 6])
        mv = sb("mv", [P, BT, 2])
        std = sb("std", [P, BT])
        rstd = sb("rstd", [P, BT])
        eps = sb("eps", [P, 1])
        ident = sb("ident", [P, P])
        ident_bf = sb("ident_bf", [P, P], BF16)
        wqkvo = [sb(f"wqkvo{i}", [P, DK, D]) for i in range(4)]
        wqo_b = [sb(f"wqo_b{i}", [P, DK, D]) for i in range(2)]
        wkv_b = [sb(f"wkv_b{i}", [P, DK, KV_HEADS * HD]) for i in range(2)]
        wg = sb("wg", [P, DK, INNER])
        wu = sb("wu", [P, DK, INNER])
        wd = sb("wd", [P, INNER // P, D])
        bqk = sb("bqk", [P, 2, DK])
        bv_rows = sb("bv_rows", [P, D])
        bo_rows = sb("bo_rows", [P, D])
        band = sb("band", [P, 2, 2 * P])
        band_out = sb("band_out", [P, 2, 2 * P])
        vsb = sb("vsb", [P, GROUPS, BT, GH * HD])
        mneg = sb("mneg", [P, HALF, CPH])
        mband = sb("mband", [P, HALF, CPH])
        mrest = sb("mrest", [P, HALF, CPH])
        mres1 = sb("mres1", [P, HALF, CPH])
        mres2 = sb("mres2", [P, HALF, CPH])
        nought = sb("nought", [P, HALF, CPH])
        mparts = sb("mparts", [P, HALF, 2, PARTS, CPH // 2], BF16)
        mT = sb("mT", [CPH * PARTS, HALF, P], BF16)
        sums = sb("sums", [P, BATCH, 2 * P])
        isums = sb("isums", [P, BATCH, 2 * P])
        area = sb("area", [P, AREA])

        def carve(at, shape, dt):
            n = 1
            for size in shape:
                n *= size
            end = at + n * (4 if dt == F32 else 2) // 4
            assert end <= AREA, end
            v = area[:, at:end]
            if dt != F32:
                v = v.bitcast(dt)
            names = "abcd"[:len(shape)]
            return v.rearrange("p (" + " ".join(names) + ") -> p " + " ".join(names),
                               **dict(zip(names, shape))), end

        probs, at = carve(0, [PRING, GH, BANK], F32)
        ctx_sb, at = carve(at, [HALF, BANK], F32)
        ones_at = at
        k_max, at = carve(at, [2, GH // 2, SEQ], BF16)
        k_st, at = carve(at, [2, GH // 2, SEQ], BF16)
        vaug_at = at
        vaug, at = carve(at, [2, BT, GH, VW], F32)
        q_st_at = at
        q_st, at = carve(at, [2, GH, SEQ], BF16)
        q_max_at = at
        q_max, at = carve(at, [2, GH, SEQ], BF16)
        q_max_end = at
        hid, at = carve(0, [2, INNER // P, BANK], F32)
        gated, at = carve(at, [2, BANK], F32)
        mag, at = carve(at, [4, BANK], F32)
        wins, at = carve(at, [6, BANK], BF16)
        tally, at = carve(at, [4, BANK], BF16)
        tally2, at = carve(at, [4, BANK], BF16)
        assert at <= q_st_at
        parts_low, _ = carve(0, [2, PARTS, SEQ], BF16)
        parts, at = carve(q_st_at, [2, PARTS, SEQ], BF16)
        parts = [parts[:, 0], parts[:, 1], parts_low[:, 0], parts_low[:, 1]]
        resid, at = carve(at, [2, BANK], F32)
        assert at <= q_max_at
        ctxn, at = carve(q_max_at, [2, DK, BANK], F32)
        inv, at = carve(at, [2, DK, BANK], F32)
        assert at <= q_max_end

        psum = ctx.enter_context(nc.psum_tensor("psum", [P, 8, BANK], F32))
        T_BANK = psum[:, 7, :].bitcast(BF16)
        PV_BANK = 6

        x_loaded = [sem(f"x_loaded{b}") for b in range(BATCH)]
        w_loaded = [sem("wa_loaded"), sem("wb_loaded")]
        wf_loaded = sem("wf_loaded")
        bias_loaded = sem("bias_loaded")
        stacks_stored = [sem(f"stacks_stored{i}") for i in range(4)]
        max_loaded = [sem(f"max_stack_loaded{i}") for i in range(2)]
        st_loaded = [sem(f"stack_loaded{i}") for i in range(2)]
        mrow_stored = sem("mrow_stored")
        mrow_loaded = sem("mrow_loaded")
        ctx_stored = sem("ctx_stored")
        sums_loaded = sem("sums_loaded")
        inv_stored = sem("inv_stored")
        ctx_loaded = [sem(f"ctx_loaded{i}") for i in range(2)]
        out_stored = sem("out_stored")
        const_ready = sem("const_ready")
        area_set = sem("area_set")
        ln_stats, ln_mv, ln_sd, ln_rstd, ln_xn = (sem(s) for s in ("ln_stats", "ln_mv", "ln_sd", "ln_rstd", "ln_xn"))
        ln_tr, ln_evac = sem("ln_tr"), sem("ln_evac")
        proj_ready, hi_done, rest_done, mid_done, lo_done = (
            sem(s) for s in ("proj_ready", "hi_done", "rest_done", "mid_done", "lo_done"))
        v_ready, v_done = sem("v_ready"), sem("v_done")
        vaug_ready = sem("vaug_ready")
        max_ready, max_used = sem("max_ready"), sem("max_used")
        cols_ready, split_done, mparts_ready = sem("cols_ready"), sem("split_done"), sem("mparts_ready")
        mT_ready, mT_copied = sem("mT_ready"), sem("mT_copied")
        st_ready, exp_done, masked, pv_done, ctx_copied = (
            sem(s) for s in ("st_ready", "exp_done", "masked", "pv_done", "ctx_copied"))
        isums_ready, ctxn_ready, o_ready = sem("isums_ready"), sem("ctxn_ready"), sem("o_ready")
        turn_started, mask_started = sem("turn_started"), sem("mask_started")
        x_biased, x_attended, x_fed = sem("x_biased"), sem("x_attended"), sem("x_fed")
        gate_ready, up_ready, silu_done, hid_done, mag_done, wins_done, tally_done, tally2_done, sparse_done, down_ready = (
            sem(s) for s in ("gate_ready", "up_ready", "silu_done", "hid_done", "mag_done", "wins_done",
                             "tally_done", "tally2_done", "sparse_done", "down_ready"))

        QUARTERS = [
            [(0, 0, P), (1, 0, P), (0, 1, P), (1, 1, P)],
            [(0, 0, P), (1, 0, KV_HEADS * HD), (0, 1, P)],
        ]
        PCH = [2 * len(q) for q in QUARTERS]
        PBASE = [0, BATCH * PCH[0]]
        VCH = [BT // 2, 1]
        VBASE = [0, BATCH * VCH[0]]
        O_BANKS = [(2, 3), (4, 5), (6, 7), (6, 7)]
        SD = 16 * len(RUNS)
        NQ = [len(q) for q in QUARTERS]
        QBASE = [0, BATCH * NQ[0]]
        w_a = [[wqkvo[0], wqkvo[1], wqkvo[2], wqkvo[3]], [wqo_b[0], wkv_b[0], wkv_b[1], wqo_b[1]]]
        STACK_DMAS = 64

        SLOT = [0, 1, 2, 3, 0, 1, 2, 3] + [0, 1, 0, 2, 3, 1]

        def stored(slot, pairs):
            return SD * SLOT[:pairs].count(slot)

        def loads(G, buf):
            return STACK_DMAS // 2 * (G - buf) + STACK_DMAS

        block = ctx.enter_context(nc.Block())

        @block.sync
        def _(sp):
            for b in range(BATCH):
                sp.dma_start(x[:, b * BT:(b + 1) * BT, :],
                             x_in[b].rearrange("(t p) d -> p t d", p=P)).then_inc(x_loaded[b], 16)
            for w, src in zip(wqkvo, (wq_a, wk_a, wv_a, wo_a)):
                sp.dma_start(w[:], src.rearrange("(k p) n -> p k n", p=P)).then_inc(w_loaded[0], 16)
            for i, src in enumerate((bq_a, bk_a)):
                sp.dma_start(bqk[:, i, :], src.rearrange("(m p) -> p m", p=P),
                             allow_slow_non_contiguous=True).then_inc(bias_loaded, 16)
            for dst, src in ((bv_rows, bv_a), (bo_rows, bo_a)):
                sp.dma_start(dst[:], src.rearrange("(o d) -> o d", o=1).to_broadcast((P, D))).then_inc(bias_loaded, 16)
            for w, src in zip((*wqo_b, *wkv_b), (wq_b, wo_b, wk_b, wv_b)):
                sp.dma_start(w[:], src.rearrange("(k p) n -> p k n", p=P)).then_inc(w_loaded[1], 16)
            for w, src in ((wg, w_gate), (wu, w_up)):
                sp.dma_start(w[:], src.rearrange("(k p) n -> p k n", p=P)).then_inc(wf_loaded, 16)
            sp.dma_start(wd[:].rearrange("p (h r) n -> p h r n", h=2),
                         w_down.rearrange("(h p r) n -> p h r n", h=2, r=4)).then_inc(wf_loaded, 16)

            def store_stacks(a, b):
                for j, (w, m, rows) in enumerate(QUARTERS[a]):
                    n = QBASE[a] + b * NQ[a] + j
                    sp.wait_ge(lo_done, PBASE[a] + b * PCH[a] + 2 * j + 2)
                    g0 = b * GPB + m * (P // HD // GH)
                    for q_part, (blk, many) in enumerate(RUNS):
                        if w == 0:
                            src = parts[SLOT[n]][0:rows, q_part:q_part + 1, :].to_broadcast((rows, many, SEQ))
                        else:
                            src = parts[SLOT[n]][0:rows, 0:many, :]
                        to = slice(blk, blk + many)
                        if a == 1 and w == 1:
                            dst = k_stacks_b[b * GPB:(b + 1) * GPB, :, to, :].rearrange("g d k t -> (g d) k t")
                        else:
                            stacks = ((q_stacks, k_stacks), (q_stacks_b, None))[a][w]
                            dst = stacks[g0:g0 + P // HD // GH, :, :, to, :].rearrange("g h d k t -> (g h d) k t")
                        sp.dma_start(dst, src).then_inc(stacks_stored[SLOT[n]], 16)
                    if b == 0 and j == 1:
                        for i in (SLOT[n - 1], SLOT[n]):
                            sp.wait_ge(stacks_stored[i], stored(i, n + 1))
                        sp.wait_ge(area_set, 5 + 2 * a)
                        load_max_stack(a, 0, 0)
                        load_max_stack(a, 1, 1)

            def load_stack(a, g, buf, q, keys, done):
                for par in range(2):
                    lo = PAR * par
                    qs = (q_stacks, q_stacks_b)[a]
                    sp.dma_start(q[lo:lo + ROWS, buf, par::2, :],
                                 qs[g, par::2].rearrange("a d k t -> (d k) a t")).then_inc(done, 16)
                    if a == 0:
                        sp.dma_start(keys[lo:lo + ROWS, buf, :, :],
                                     k_stacks[g, par::2].rearrange("a d k t -> (d k) a t")).then_inc(done, 16)
                    else:
                        sp.dma_start(keys[lo:lo + ROWS, buf, 0, :],
                                     k_stacks_b[g].rearrange("d k t -> (d k) t")).then_inc(done, 16)

            def load_max_stack(a, g, buf):
                if not isinstance(g, int) or g >= 2 or a:
                    sp.wait_ge(max_ready, CHUNKS * (GROUPS * a + g - 1))
                load_stack(a, g, buf, q_max, k_max, max_loaded[buf])

            def load_st_stack(a, g, buf):
                if not isinstance(g, int) or g >= 2 or a:
                    sp.wait_ge(st_ready, GH * UNITS * (GROUPS * a + g - 1))
                load_stack(a, g, buf, q_st, k_st, st_loaded[buf])

            def move_max(a, g, buf, qh):
                n = HALF * (GROUPS * a + g) + qh
                sp.wait_ge(mT_copied, n + 1)
                if not isinstance(g, int) or n >= 4:
                    sp.wait_ge(mrow_loaded, 32 * (n - 3))
                sp.dma_start(max_rows[buf, qh].rearrange("a c (i t) -> (a c i) t", t=P),
                             mT[:, qh, :]).then_inc(mrow_stored, 16)
                sp.wait_ge(mrow_stored, 16 * (n + 1))
                for par in range(2):
                    lo = PAR * par + MROW
                    sp.dma_start(q_st[lo:lo + PARTS, buf, par::2, qh * BANK:(qh + 1) * BANK],
                                 max_rows[buf, qh, par].rearrange("c (i t) -> c i t", i=GH // 2)
                                 ).then_inc(mrow_loaded, 16)

            def store_ctx(a, g, qh):
                sp.wait_ge(ctx_copied, HALF * (GROUPS * a + g) + qh + 1)
                sp.dma_start(ctx_rows[a][g, :, :, qh * BANK:(qh + 1) * BANK], ctx_sb[:, qh, :]).then_inc(ctx_stored, 16)

            def group(a, g, buf, first=False, ahead=2):
                if ahead >= 1:
                    load_st_stack(a, g + 1, 1 - buf)
                if not first:
                    store_ctx(a, g - 1, 1)
                if ahead >= 2:
                    load_max_stack(a, g + 2, buf)
                move_max(a, g, buf, 1)
                store_ctx(a, g, 0)
                if ahead >= 1:
                    move_max(a, g + 1, 1 - buf, 0)

            def store_inverses(a, b):
                sp.dma_start(sums[:, b, :],
                             ctx_rows[a][b * GPB:(b + 1) * GPB, :, HD, :].rearrange(
                                 "g i (s c) -> g i s c", c=2 * P)).then_inc(sums_loaded, 16)
                sp.wait_ge(isums_ready, BATCH * a + b + 1)
                sp.dma_start(inv_rows[a][b].rearrange("h (s c) -> h s c", c=2 * P),
                             isums[:, b, :]).then_inc(inv_stored, 16)
                sp.wait_ge(inv_stored, 16 * (BATCH * a + b + 1))

            def load_ctx(a, b):
                for c in (HALF * b, HALF * b + 1):
                    qh = c % HALF
                    if c >= 2:
                        sp.wait_ge(o_ready, 8 * a + 2 * (c - 1))
                    for m in range(DK):
                        g0 = b * GPB + m * (GPB // DK)
                        hs = HEADS // DK
                        sp.dma_start(ctxn[:, c % 2, m, :],
                                     ctx_rows[a][g0:g0 + GPB // DK, :, 0:HD, qh * BANK:(qh + 1) * BANK]
                                     ).then_inc(ctx_loaded[c % 2], 16)
                        sp.dma_start(inv[:, c % 2, m, :],
                                     inv_rows[a][b, m * hs:(m + 1) * hs, qh * BANK:(qh + 1) * BANK].rearrange(
                                         "h (o t) -> h o t", o=1).to_broadcast((hs, HD, BANK))
                                     ).then_inc(ctx_loaded[c % 2], 16)

            for a in range(2):
                store_stacks(a, 0)
                store_stacks(a, 1)
                for i in range(4):
                    sp.wait_ge(stacks_stored[i], stored(i, QBASE[a] + BATCH * NQ[a]))
                sp.wait_ge(area_set, 6 + 2 * a)
                load_st_stack(a, 0, 0)
                move_max(a, 0, 0, 0)
                group(a, 0, 0, first=True)
                with sp.Fori(0, GPB // 2) as i:
                    group(a, 2 * i + 1, 1)
                    group(a, 2 * i + 2, 0)
                sp.wait_ge(ctx_stored, 16 * (HALF * (GROUPS * a + GPB) + 1))
                store_inverses(a, 0)
                with sp.Fori(GPB // 2, (GROUPS - 4) // 2) as i:
                    group(a, 2 * i + 1, 1)
                    group(a, 2 * i + 2, 0)
                group(a, GROUPS - 3, 1)
                group(a, GROUPS - 2, 0, ahead=1)
                sp.wait_ge(max_ready, CHUNKS * GROUPS * (a + 1))
                load_ctx(a, 0)
                group(a, GROUPS - 1, 1, ahead=0)
                store_ctx(a, GROUPS - 1, 1)
                sp.wait_ge(ctx_stored, 16 * HALF * GROUPS * (a + 1))
                store_inverses(a, 1)
                load_ctx(a, 1)
            for c in range(TILES // 2):
                sp.wait_ge(x_fed, 8 + c + 1)
                b, t = divmod(2 * c, BT)
                sp.dma_start(out[b, t * P:(t + 2) * P, :].rearrange("(t p) d -> p t d", p=P),
                             x[:, 2 * c:2 * c + 2, :]).then_inc(out_stored, 16)
            sp.wait_ge(out_stored, 16 * (TILES // 2))

        @block.tensor
        def _(pe):
            def norm_transpose(k, b):
                n = 2 * k + b
                for tp in range(BT // 2):
                    pe.wait_ge(ln_xn, BT * n + 2 * tp + 2)
                    if 4 * n + tp >= 2:
                        pe.wait_ge(ln_evac, 4 * n + tp - 1)
                    for t in range(2):
                        for d in range(DK):
                            mm = pe.transpose(psum[:, 6 + tp % 2, (t * DK + d) * P:(t * DK + d + 1) * P],
                                              xn[:, 2 * tp + t, d * P:(d + 1) * P], ident[:])
                    mm.then_inc(ln_tr, 1)

            def project(a, b):
                pe.wait_ge(w_loaded[a], 64)
                pe.wait_ge(ln_evac, 4 * (4 * a + b) + 4)
                if a == 1:
                    pe.wait_ge(hid_done, 28 + 4 * b)
                for j, (w, m, rows) in enumerate(QUARTERS[a]):
                    for half in range(HALF):
                        n = PBASE[a] + b * PCH[a] + 2 * j + half
                        if n >= 4:
                            pe.wait_ge(rest_done, n - 3)
                        for k in range(DK):
                            mm = pe.matmul(psum[0:rows, n % 4, :], w_a[a][w][:, k, m * P:m * P + rows],
                                           xnT[:, k, b * SEQ + half * BANK:b * SEQ + (half + 1) * BANK],
                                           start=(k == 0), stop=(k == DK - 1))
                        mm.then_inc(proj_ready, 1)
                if a == 1:
                    pe.wait_ge(x_fed, 6 + 2 * b)
                width = (D, KV_HEADS * HD)[a]
                per = BANK // width
                for v in range(VCH[a]):
                    n = VBASE[a] + b * VCH[a] + v
                    if n >= 2:
                        pe.wait_ge(v_done, n - 1)
                    for t in range(per):
                        tok = b * SEQ + (v * per + t) * P
                        for k in range(DK):
                            mm = pe.matmul(psum[:, 4 + n % 2, t * width:(t + 1) * width], xnT[:, k, tok:tok + P],
                                           w_a[a][2][:, k, :], start=(k == 0), stop=(k == DK - 1))
                    mm.then_inc(v_ready, 1)

            def max_scores(a, g, buf, c, split=False):
                qh, r = divmod(c, CPH)
                head, qt = divmod(r, BT // HALF)
                tile, n = qh * (BT // HALF) + qt, CHUNKS * (GROUPS * a + g) + c
                if c == 0:
                    pe.wait_ge(max_loaded[buf], loads(GROUPS * a + g, buf))
                if not isinstance(g, int) or n >= 2:
                    pe.wait_ge(max_used, n - 1)
                q = q_max[:, buf, head, tile * P:(tile + 1) * P]
                keys = k_max[:, buf, 0 if a else head // 2, :]
                slot = psum[:, 2 + 2 * (c % 2):4 + 2 * (c % 2), :].rearrange("p b c -> p (b c)")
                if a == 0:
                    pieces = [(0, 0, BANK), (BANK, BANK, BANK)]
                else:
                    pieces, at = [], 0
                    while at < SEQ:
                        key = ((tile - 1) * P + at) % SEQ
                        size = min(BANK - at % BANK, SEQ - key)
                        pieces.append((at, key, size))
                        at += size

                def multiply(some):
                    for at, key, size in some:
                        mm = pe.matmul(slot[:, at:at + size], q, keys[:, key:key + size], start=True, stop=True,
                                       skip_group_check=True)
                    return mm

                def rest():
                    multiply([p for p in pieces if p[0] >= BANK]).then_inc(max_ready, 1)

                multiply([p for p in pieces if p[0] < BANK])
                if split:
                    return rest
                rest()

            def turn_max(a, g, qh):
                n = HALF * (GROUPS * a + g) + qh
                pe.wait_ge(mparts_ready, n + 1)
                if not isinstance(g, int) or n >= 1:
                    pe.wait_ge(mT_copied, n)
                pe.sem_inc(turn_started, 1)
                pe.transpose(T_BANK[0:CPH * PARTS, 0:P], mparts[:, qh].rearrange("p a c i -> p (a c i)"),
                             ident_bf[:]).then_inc(mT_ready, 1)

            def scores(a, g, buf, u, head):
                qh, kt = divmod(u, BT)
                n = GH * (UNITS * (GROUPS * a + g) + u) + head
                if head == 0 and u == 0:
                    pe.wait_ge(st_loaded[buf], loads(GROUPS * a + g, buf))
                if head == 0 and kt == 0:
                    pe.wait_ge(mrow_loaded, 32 * (HALF * (GROUPS * a + g) + qh + 1))
                if not isinstance(g, int) or n >= 2:
                    pe.wait_ge(exp_done, n - 1)
                pe.matmul(psum[:, head % 2, :],
                          k_st[:, buf, 0 if a else head // 2, kt * P:(kt + 1) * P],
                          q_st[:, buf, head, qh * BANK:(qh + 1) * BANK],
                          start=True, stop=True).then_inc(st_ready, 1)

            def times_v(a, g, buf, u):
                qh, kt = divmod(u, BT)
                if a == 1 and u in MASKED_UNITS:
                    pe.wait_ge(masked, MPG * g + MASKED_UNITS.index(u) + 1)
                else:
                    pe.wait_ge(exp_done, GH * (UNITS * (GROUPS * a + g) + u + 1))
                if u == 0:
                    pe.wait_ge(vaug_ready, GROUPS * a + g + 1)
                if kt == 0 and (not isinstance(g, int) or HALF * (GROUPS * a + g) + qh > 0):
                    pe.wait_ge(ctx_copied, HALF * (GROUPS * a + g) + qh)
                for head in range(GH):
                    mm = pe.matmul(psum[head * VW:(head + 1) * VW, PV_BANK, :], vaug[:, buf, kt, head, :],
                                   probs[:, u % PRING, head, :], start=(kt == 0), stop=(kt == BT - 1))
                mm.then_inc(pv_done, 1)

            def group(a, g, buf, first=False, ahead=True):
                for u in range(UNITS):
                    if u == 5:
                        turn_max(a, g, 1)
                    if u == 13 and ahead:
                        turn_max(a, g + 1, 0)
                    scores(a, g, buf, u, 0)
                    scores(a, g, buf, u, 1)
                    if not ahead and u >= UNITS - BT:
                        project_tile(a, u - (UNITS - BT))
                    second, c = None, 2 * u + LEAD
                    if c < CHUNKS:
                        max_scores(a, g, buf, c)
                        second = max_scores(a, g, buf, c + 1, split=True)
                    elif ahead:
                        max_scores(a, g + 1, 1 - buf, c - CHUNKS)
                        second = max_scores(a, g + 1, 1 - buf, c + 1 - CHUNKS, split=True)
                    scores(a, g, buf, u, 2)
                    if second:
                        second()
                    scores(a, g, buf, u, 3)
                    if u:
                        times_v(a, g, buf, u - 1)
                    elif not first:
                        times_v(a, g - 1, 1 - buf, UNITS - 1)

            def project_tile(a, tile):
                c, t = divmod(tile, 4)
                pair = t // 2
                if t == 0:
                    pe.wait_ge(ctxn_ready, 4 * a + c + 1)
                if c == 3 and t % 2 == 0:
                    pe.wait_ge(x_attended, 8 * a + 4 + pair + 1)
                for m in range(DK):
                    mm = pe.matmul(psum[:, O_BANKS[c][pair], t % 2 * D:(t % 2 + 1) * D],
                                   ctxn[:, c % 2, m, t * P:(t + 1) * P], w_a[a][3][:, m, :],
                                   start=(m == 0), stop=(m == DK - 1))
                if t % 2:
                    mm.then_inc(o_ready, 1)

            def project_out(a, c):
                for t in range(4):
                    project_tile(a, 4 * c + t)

            def gate_up(f, c, h):
                pe.wait_ge(ln_evac, 4 * (2 * (2 * f + 1) + c // HALF) + 4)
                if f == 0 and c == 3 and h == 1:
                    pe.wait_ge(rest_done, PBASE[1] + PCH[1])
                for r in range(4):
                    n = 32 * f + 8 * c + 4 * h + r
                    cols = slice(h * 4 * P + r, (h + 1) * 4 * P, 4)
                    for w, base, done in ((wg, 0, gate_ready), (wu, 2, up_ready)):
                        if n >= 2:
                            pe.wait_ge(hid_done, n - 1)
                        for k in range(DK):
                            mm = pe.matmul(psum[:, base + r % 2, :], w[:, k, cols],
                                           xnT[:, k, c * BANK:(c + 1) * BANK], start=(k == 0), stop=(k == DK - 1))
                        mm.then_inc(done, 1)

            def down(f, c, first=0, last=INNER // P - 1):
                half = INNER // P // 2
                pe.wait_ge(sparse_done, 8 * f + 2 * c + last // half + 1)
                if f == 0 and c == 3 and first == 0:
                    pe.wait_ge(v_done, VBASE[1] + VCH[1])
                for pair in range(2):
                    if c and first == 0:
                        pe.wait_ge(x_fed, 8 * f + 2 * (c - 1) + pair + 1)
                    for t in range(2):
                        tok = (2 * pair + t) * P
                        to = psum[:, 4 + 2 * pair + t, 0:D] if c == 3 else psum[:, 4 + pair, t * D:(t + 1) * D]
                        for i in range(first, last + 1):
                            mm = pe.matmul(to, hid[:, c % 2, i, tok:tok + P], wd[:, i, :],
                                           start=(i == 0), stop=(i == INNER // P - 1))
                    if last == INNER // P - 1:
                        mm.then_inc(down_ready, 1)

            def attend(a):
                pe.wait_ge(rest_done, PBASE[a] + BATCH * PCH[a])
                pe.wait_ge(v_done, VBASE[a] + BATCH * VCH[a])
                for c in range(LEAD):
                    if c == CPH + 3:
                        turn_max(a, 0, 0)
                    max_scores(a, 0, 0, c)
                group(a, 0, 0, first=True)
                with pe.Fori(0, (GROUPS - 2) // 2) as i:
                    group(a, 2 * i + 1, 1)
                    group(a, 2 * i + 2, 0)
                group(a, GROUPS - 1, 1, ahead=False)
                times_v(a, GROUPS - 1, 1, UNITS - 1)

            pe.wait_ge(const_ready, 1)
            for b in range(BATCH):
                norm_transpose(0, b)
            for b in range(BATCH):
                project(0, b)
            for a in range(2):
                attend(a)
                pe.wait_ge(ctx_copied, HALF * GROUPS * (a + 1))
                norm_transpose(2 * a + 1, 0)
                if a == 0:
                    pe.wait_ge(wf_loaded, 48)
                gate_up(a, 0, 0)
                gate_up(a, 0, 1)
                project_out(a, 2)
                gate_up(a, 1, 0)
                project_out(a, 3)
                down(a, 0)
                gate_up(a, 1, 1)
                norm_transpose(2 * a + 1, 1)
                gate_up(a, 2, 0)
                down(a, 1)
                gate_up(a, 2, 1)
                gate_up(a, 3, 0)
                down(a, 2)
                if a == 0:
                    norm_transpose(2, 0)
                    project(1, 0)
                gate_up(a, 3, 1)
                down(a, 3, last=INNER // P // 2 - 1)
                down(a, 3, first=INNER // P // 2)
                if a == 0:
                    norm_transpose(2, 1)
                    project(1, 1)

        @block.scalar
        def _(act):
            def norm(k, b):
                n = 2 * k + b
                act.wait_ge(ln_mv, n + 1)
                if n == 0:
                    act.wait_ge(const_ready, 1)
                act.activation(std[:], mv[:, :, 1], ACT.Sqrt, bias=eps[:]).then_inc(ln_sd, 1)

            def copy_transposed(k, b):
                n = 2 * k + b
                for tp in range(BT // 2):
                    act.wait_ge(ln_tr, 4 * n + tp + 1)
                    act.copy(xnT[:, :, (b * BT + 2 * tp) * P:(b * BT + 2 * tp + 2) * P].rearrange(
                        "p d (t c) -> p d t c", t=2),
                        psum[:, 6 + tp % 2, :].rearrange("p (t d c) -> p d t c", t=2, d=DK)).then_inc(ln_evac, 1)

            def split(a, b):
                for i in range(PCH[a] + 1):
                    if i < PCH[a]:
                        j, half = divmod(i, HALF)
                        w, m, rows = QUARTERS[a][j]
                        n, s = PBASE[a] + b * PCH[a] + i, QBASE[a] + b * NQ[a] + j
                        if SLOT[s] in SLOT[:s] and half == 0:
                            act.wait_ge(stacks_stored[SLOT[s]], stored(SLOT[s], s))
                        act.wait_ge(proj_ready, n + 1)
                        dst = parts[SLOT[s]][0:rows, 0, half * BANK:(half + 1) * BANK]
                        if a == 0:
                            act.activation(dst, psum[0:rows, n % 4, :], ACT.Identity,
                                           bias=bqk[:, w, m:m + 1]).then_inc(hi_done, 1)
                        else:
                            act.copy(dst, psum[0:rows, n % 4, :]).then_inc(hi_done, 1)
                    if i:
                        j, half = divmod(i - 1, HALF)
                        w, m, rows = QUARTERS[a][j]
                        n, s = PBASE[a] + b * PCH[a] + i - 1, QBASE[a] + b * NQ[a] + j
                        act.wait_ge(rest_done, n + 1)
                        act.copy(parts[SLOT[s]][0:rows, 1, half * BANK:(half + 1) * BANK],
                                 resid[0:rows, n % 2, :]).then_inc(mid_done, 1)

            def exps(a, g, u):
                G = GROUPS * a + g
                if not isinstance(g, int) or UNITS * G + u >= PRING:
                    act.wait_ge(pv_done, UNITS * G + u - PRING + 1)
                for head in range(GH):
                    act.wait_ge(st_ready, GH * (UNITS * G + u) + head + 1)
                    act.activation(probs[:, u % PRING, head, :], psum[:, head % 2, :], ACT.Exp,
                                   scale=SCALE).then_inc(exp_done, 1)

            def copy_ctx(a, g, qh):
                n = HALF * (GROUPS * a + g) + qh
                act.wait_ge(pv_done, UNITS * (GROUPS * a + g) + (qh + 1) * BT)
                if not isinstance(g, int) or n >= 2:
                    act.wait_ge(ctx_stored, 16 * (n - 1))
                act.copy(ctx_sb[:, qh, :], psum[:, PV_BANK, :]).then_inc(ctx_copied, 1)

            def group(a, g, first=False):
                for u in range(UNITS):
                    exps(a, g, u)
                    if u == 0 and not first:
                        copy_ctx(a, g - 1, 1)
                    if u == BT:
                        copy_ctx(a, g, 0)

            def silu_and_size(f, c, h):
                if c == 0 and h == 0:
                    act.wait_ge(ctx_stored, 16 * HALF * GROUPS * (f + 1))
                for r in range(5):
                    n = 32 * f + 8 * c + 4 * h + r
                    if r < 4:
                        act.wait_ge(gate_ready, n + 1)
                        if n >= 2:
                            act.wait_ge(hid_done, n - 1)
                        act.activation(gated[:, r % 2, :], psum[:, r % 2, :], ACT.Silu).then_inc(silu_done, 1)
                    if r:
                        act.wait_ge(hid_done, n)
                        if r == 1 and 8 * f + 2 * c + h:
                            act.wait_ge(wins_done, 3 * (8 * f + 2 * c + h))
                        act.activation(mag[:, r - 1, :], hid[:, c % 2, 4 * h + r - 1, :],
                                       ACT.Abs).then_inc(mag_done, 1)

            def attend(a):
                for i in range(4):
                    act.wait_ge(stacks_stored[i], stored(i, QBASE[a] + BATCH * NQ[a]))
                group(a, 0, first=True)
                with act.Fori(0, (GROUPS - 2) // 2) as i:
                    group(a, 2 * i + 1)
                    group(a, 2 * i + 2)
                group(a, GROUPS - 1)
                copy_ctx(a, GROUPS - 1, 1)

            for b in range(BATCH):
                norm(0, b)
                copy_transposed(0, b)
            act.wait_ge(bias_loaded, 64)
            for b in range(BATCH):
                split(0, b)
            for a in range(2):
                attend(a)
                norm(2 * a + 1, 0)
                copy_transposed(2 * a + 1, 0)
                silu_and_size(a, 0, 0)
                silu_and_size(a, 0, 1)
                silu_and_size(a, 1, 0)
                norm(2 * a + 1, 1)
                silu_and_size(a, 1, 1)
                copy_transposed(2 * a + 1, 1)
                silu_and_size(a, 2, 0)
                silu_and_size(a, 2, 1)
                silu_and_size(a, 3, 0)
                if a == 0:
                    norm(2, 0)
                    copy_transposed(2, 0)
                    split(1, 0)
                silu_and_size(a, 3, 1)
                if a == 0:
                    norm(2, 1)
                    copy_transposed(2, 1)
                    split(1, 1)

        @block.vector
        def _(dve):
            def norm(k, b):
                n = 2 * k + b
                if k == 0:
                    dve.wait_ge(x_loaded[b], 16)
                elif k % 2:
                    dve.wait_ge(x_attended, 8 * (k // 2) + 4 * (b + 1))
                else:
                    dve.wait_ge(x_fed, 4 * (b + 1))
                if n:
                    dve.wait_ge(ln_xn, BT * n)
                for t in range(BT):
                    ins = dve.bn_stats(stats[:, t, :], x[:, b * BT + t, :])
                ins.then_inc(ln_stats, 1)
                dve.wait_ge(ln_stats, n + 1)
                for t in range(BT):
                    ins = dve.bn_aggr(mv[:, t, :], stats[:, t, :])
                ins.then_inc(ln_mv, 1)
                dve.wait_ge(ln_sd, n + 1)
                dve.reciprocal(rstd[:], std[:]).then_inc(ln_rstd, 1)
                dve.wait_ge(ln_rstd, n + 1)
                for t in range(BT):
                    if n and t % 2 == 0:
                        dve.wait_ge(ln_tr, 4 * (n - 1) + t // 2 + 1)
                    dve.tensor_scalar(xn[:, t, :], x[:, b * BT + t, :], mv[:, t, 0:1], rstd[:, t:t + 1],
                                      ALU.subtract, ALU.mult).then_inc(ln_xn, 1)

            def copy_v(a, b):
                for v in range(VCH[a]):
                    n = VBASE[a] + b * VCH[a] + v
                    dve.wait_ge(v_ready, n + 1)
                    bank = psum[:, 4 + n % 2, :]
                    if a == 0:
                        dve.tensor_tensor(
                            vsb[:, b * GPB:(b + 1) * GPB, 2 * v:2 * v + 2, :].rearrange("p g k c -> p k g c"),
                            bank.rearrange("p (k g c) -> p k g c", k=2, g=GPB),
                            bv_rows[:].rearrange("p (o g c) -> p o g c", o=1, g=GPB).to_broadcast((P, 2, GPB, GH * HD)),
                            ALU.add).then_inc(v_done, 1)
                    else:
                        dve.tensor_copy(
                            vsb[:, b * GPB:(b + 1) * GPB, :, 0:HD].rearrange("p g k c -> p k g c"),
                            bank.rearrange("p (k g c) -> p k g c", k=BT, g=GPB)).then_inc(v_done, 1)

            def split(a, b):
                for i in range(PCH[a] + 1):
                    if i < PCH[a]:
                        j, half = divmod(i, HALF)
                        w, m, rows = QUARTERS[a][j]
                        n, s = PBASE[a] + b * PCH[a] + i, QBASE[a] + b * NQ[a] + j
                        dve.wait_ge(hi_done, n + 1)
                        hi = parts[SLOT[s]][0:rows, 0, half * BANK:(half + 1) * BANK]
                        if n >= 2:
                            dve.wait_ge(lo_done, n - 1)
                        if a == 0:
                            dve.scalar_tensor_tensor(out=resid[0:rows, n % 2, :], in0=psum[0:rows, n % 4, :],
                                                     scalar=bqk[:, w, m:m + 1], in1=hi, op0=ALU.add,
                                                     op1=ALU.subtract).then_inc(rest_done, 1)
                        else:
                            dve.tensor_tensor(resid[0:rows, n % 2, :], psum[0:rows, n % 4, :], hi,
                                              ALU.subtract).then_inc(rest_done, 1)
                    if i:
                        j, half = divmod(i - 1, HALF)
                        w, m, rows = QUARTERS[a][j]
                        n, s = PBASE[a] + b * PCH[a] + i - 1, QBASE[a] + b * NQ[a] + j
                        dve.wait_ge(mid_done, n + 1)
                        dve.tensor_tensor(parts[SLOT[s]][0:rows, 2, half * BANK:(half + 1) * BANK],
                                          resid[0:rows, n % 2, :],
                                          parts[SLOT[s]][0:rows, 1, half * BANK:(half + 1) * BANK],
                                          ALU.subtract).then_inc(lo_done, 1)
                copy_v(a, b)

            def maxima(a, g, c):
                qh, r = divmod(c, CPH)
                head, qt = divmod(r, BT // HALF)
                G = GROUPS * a + g
                col = (head % 2) * (CPH // 2) + (head // 2) * (BT // HALF) + qt
                if r == 0 and (not isinstance(g, int) or G >= 1):
                    dve.wait_ge(mparts_ready, HALF * (G - 1) + qh + 1)
                dve.wait_ge(max_ready, CHUNKS * G + c + 1)
                slot = psum[:, 2 + 2 * (c % 2):4 + 2 * (c % 2), :].rearrange("p b c -> p (b c)")
                if a == 0:
                    dve.tensor_reduce(mneg[:, qh, col:col + 1], slot, AX.X, ALU.max, negate=True).then_inc(max_used, 1)
                else:
                    if not isinstance(g, int) or c >= 2 or g:
                        dve.wait_ge(max_used, CHUNKS * G + c - 1)
                    later = 1 if qh * (BT // HALF) + qt else 0
                    dve.tensor_reduce(mrest[:, qh, col:col + 1], slot[:, 2 * P:SEQ], AX.X, ALU.max, negate=True)
                    dve.tensor_tensor_reduce(band_out[:, c % 2, :], slot[:, 0:2 * P], band[:, later, :], 1.0, -3.0e38,
                                             ALU.add, ALU.max, mband[:, qh, col:col + 1]).then_inc(max_used, 1)
                    if r == CPH - 1:
                        dve.wait_ge(max_used, CHUNKS * G + c + 1)
                        dve.scalar_tensor_tensor(out=mneg[:, qh, :], in0=mband[:, qh, :], scalar=-1.0,
                                                 in1=mrest[:, qh, :], op0=ALU.mult, op1=ALU.min).then_inc(cols_ready, 1)

            def copy_turned(a, g, qh):
                n = HALF * (GROUPS * a + g) + qh
                dve.wait_ge(mT_ready, n + 1)
                if not isinstance(g, int) or n >= 2:
                    dve.wait_ge(mrow_stored, 16 * (n - 1))
                dve.tensor_copy(mT[:, qh, :], T_BANK[0:CPH * PARTS, 0:P]).then_inc(mT_copied, 1)

            def group(a, g, ahead=True):
                for u in range(UNITS):
                    for c in (2 * u + LEAD, 2 * u + 1 + LEAD):
                        if c < CHUNKS:
                            maxima(a, g, c)
                        elif ahead:
                            maxima(a, g + 1, c - CHUNKS)
                    if u == 4:
                        copy_turned(a, g, 1)
                    if u == 12 and ahead:
                        copy_turned(a, g + 1, 0)

            def invert_sums(a, b):
                dve.wait_ge(sums_loaded, 16 * (BATCH * a + b + 1))
                dve.reciprocal(isums[:, b, :], sums[:, b, :]).then_inc(isums_ready, 1)

            def divide_ctx(a, c):
                dve.wait_ge(ctx_loaded[c % 2], 64 * (2 * a + c // 2 + 1))
                dve.tensor_tensor(ctxn[:, c % 2], ctxn[:, c % 2], inv[:, c % 2], ALU.mult).then_inc(ctxn_ready, 1)

            def add_attention(a, c):
                for pair in range(2):
                    n = 2 * c + pair
                    dve.wait_ge(o_ready, 8 * a + n + 1)
                    xs = x[:, 2 * n:2 * n + 2, :].rearrange("p t d -> p (t d)")
                    dve.tensor_tensor(xs, psum[:, O_BANKS[c][pair], :], xs, ALU.add).then_inc(x_attended, 1)

            def hidden(f, c, h):
                n0 = 8 * f + 2 * c + h
                if c >= 2 and h == 0:
                    dve.wait_ge(down_ready, 8 * f + 2 * (c - 1))
                for r in range(4):
                    n = 4 * n0 + r
                    dve.wait_ge(up_ready, n + 1)
                    dve.wait_ge(silu_done, n + 1)
                    dve.tensor_tensor(hid[:, c % 2, 4 * h + r, :], psum[:, 2 + r % 2, :], gated[:, r % 2, :],
                                      ALU.mult).then_inc(hid_done, 1)
                dve.wait_ge(mag_done, 4 * (n0 + 1))
                if n0:
                    dve.wait_ge(tally2_done, 4 * n0)
                for lo, w0, w1 in ((0, 0, 3), (1, 3, 5), (2, 5, 6)):
                    k = w1 - w0
                    dve.tensor_tensor(wins[:, w0:w1, :], mag[:, lo:lo + 1, :].to_broadcast((P, k, BANK)),
                                      mag[:, lo + 1:4, :], ALU.is_ge).then_inc(wins_done, 1)
                dve.wait_ge(wins_done, 3 * (n0 + 1))
                if n0:
                    dve.wait_ge(sparse_done, n0)
                for r, (i, j, op) in enumerate(((0, 1, ALU.add), (3, 4, ALU.add), (5, 1, ALU.subtract),
                                                (2, 4, ALU.add))):
                    dve.tensor_tensor(tally[:, r, :], wins[:, i, :], wins[:, j, :], op).then_inc(tally_done, 1)
                for r, (i, op) in enumerate(((2, ALU.add), (0, ALU.subtract), (3, ALU.subtract), (5, ALU.add))):
                    dve.wait_ge(tally_done, 4 * n0 + r + 1)
                    dve.tensor_tensor(tally2[:, r, :], tally[:, r, :], wins[:, i, :], op).then_inc(tally2_done, 1)
                for r, (need, op) in enumerate(((2.0, ALU.is_ge), (1.0, ALU.is_ge), (0.0, ALU.is_ge),
                                                (1.0, ALU.is_le))):
                    dve.wait_ge(tally2_done, 4 * n0 + r + 1)
                    ins = dve.scalar_tensor_tensor(out=hid[:, c % 2, 4 * h + r, :], in0=tally2[:, r, :], scalar=need,
                                                   in1=hid[:, c % 2, 4 * h + r, :], op0=op, op1=ALU.mult)
                ins.then_inc(sparse_done, 1)

            def add_down(f, c):
                for pair in range(2):
                    dve.wait_ge(down_ready, 8 * f + 2 * c + pair + 1)
                    xs = x[:, 4 * c + 2 * pair:4 * c + 2 * pair + 2, :]
                    if c == 3:
                        down_product = psum[:, 4 + 2 * pair:6 + 2 * pair, 0:D]
                    else:
                        down_product = psum[:, 4 + pair, :].rearrange("p (t d) -> p t d", t=2)
                    dve.tensor_tensor(xs, down_product, xs, ALU.add).then_inc(x_fed, 1)

            def attend(a):
                for c in range(LEAD):
                    maxima(a, 0, c)
                    if c == CPH + 2:
                        copy_turned(a, 0, 0)
                group(a, 0)
                with dve.Fori(0, GPB // 2) as i:
                    group(a, 2 * i + 1)
                    group(a, 2 * i + 2)
                invert_sums(a, 0)
                with dve.Fori(GPB // 2, (GROUPS - 2) // 2) as i:
                    group(a, 2 * i + 1)
                    group(a, 2 * i + 2)
                group(a, GROUPS - 1, ahead=False)
                divide_ctx(a, 0)
                divide_ctx(a, 1)

            for b in range(BATCH):
                norm(0, b)
            dve.wait_ge(bias_loaded, 64)
            for b in range(BATCH):
                split(0, b)
            for a in range(2):
                attend(a)
                if a == 0:
                    dve.wait_ge(x_biased, 1)
                add_attention(a, 0)
                add_attention(a, 1)
                norm(2 * a + 1, 0)
                invert_sums(a, 1)
                hidden(a, 0, 0)
                divide_ctx(a, 2)
                divide_ctx(a, 3)
                hidden(a, 0, 1)
                add_attention(a, 2)
                hidden(a, 1, 0)
                add_attention(a, 3)
                norm(2 * a + 1, 1)
                add_down(a, 0)
                hidden(a, 1, 1)
                hidden(a, 2, 0)
                add_down(a, 1)
                hidden(a, 2, 1)
                hidden(a, 3, 0)
                if a == 0:
                    norm(2, 0)
                add_down(a, 2)
                if a == 0:
                    split(1, 0)
                hidden(a, 3, 1)
                add_down(a, 3)
                if a == 0:
                    norm(2, 1)
                    split(1, 1)

        @block.gpsimd
        def _(pool):
            pool.memset(ident[:], 0.0).then_inc(area_set, 1)
            pool.wait_ge(area_set, 1)
            pool.affine_select(out=ident[:], in_=ident[:], compare_op=ALU.not_equal, fill=1.0, base=0,
                               pattern=[[-1, P]], channel_multiplier=1).then_inc(split_done, 1)
            pool.wait_ge(split_done, 1)
            pool.tensor_copy(ident_bf[:], ident[:])
            pool.memset(nought[:], 0.0)
            pool.memset(eps[:], EPS).then_inc(const_ready, 1)

            def extend_v(a, g, buf):
                G = GROUPS * a + g
                if not isinstance(g, int) or g >= 2:
                    pool.wait_ge(pv_done, UNITS * (G - 1))
                if isinstance(g, int) and g == 0:
                    pool.wait_ge(v_done, VBASE[a] + BATCH * VCH[a])
                pool.wait_ge(area_set, 6 + 2 * a)
                src = vsb[:, g, :, 0:(GH * HD, HD)[a]]
                if a == 0:
                    src = src.rearrange("p k (h d) -> p k h d", d=HD)
                else:
                    src = src.rearrange("p k (h d) -> p k h d", h=1).to_broadcast((P, BT, GH, HD))
                pool.tensor_copy(vaug[:, buf, :, :, 0:HD], src).then_inc(vaug_ready, 1)

            def split_max(a, g, qh):
                G = GROUPS * a + g
                n = HALF * G + qh
                if a == 0:
                    pool.wait_ge(max_used, CHUNKS * G + CPH * (qh + 1))
                else:
                    pool.wait_ge(cols_ready, HALF * g + qh + 1)
                if not isinstance(g, int) or n >= 2:
                    pool.wait_ge(mT_ready, n - 1)

                def view(t):
                    return t[:, qh, :].rearrange("p (a i) -> p a i", a=2)

                s0 = 1 + 4 * n
                pool.tensor_tensor(mparts[:, qh, :, 0, :], view(mneg), view(nought), ALU.add).then_inc(split_done, 1)
                pool.wait_ge(split_done, s0 + 1)
                pool.tensor_tensor(view(mres1), view(mneg), mparts[:, qh, :, 0, :],
                                   ALU.subtract).then_inc(split_done, 1)
                pool.wait_ge(split_done, s0 + 2)
                pool.tensor_tensor(mparts[:, qh, :, 1, :], view(mres1), view(nought), ALU.add).then_inc(split_done, 1)
                pool.wait_ge(split_done, s0 + 3)
                pool.tensor_tensor(view(mres2), view(mres1), mparts[:, qh, :, 1, :],
                                   ALU.subtract).then_inc(split_done, 1)
                pool.wait_ge(split_done, s0 + 4)
                pool.tensor_tensor(mparts[:, qh, :, 2, :], view(mres2), view(nought), ALU.add).then_inc(mparts_ready, 1)

            def mask_probs(a, g, u):
                pool.wait_ge(exp_done, GH * (UNITS * (GROUPS * a + g) + u + 1))
                pool.sem_inc(mask_started, 1)
                for kind, tile in masked_blocks(u):
                    v = probs[:, u % PRING, :, tile * P:(tile + 1) * P]
                    if kind == 0:
                        ins = pool.affine_select(out=v, in_=v, compare_op=ALU.is_ge, fill=0.0, base=0,
                                                 pattern=[[0, GH], [-1, P]], channel_multiplier=1)
                    else:
                        ins = pool.affine_select(out=v, in_=v, compare_op=ALU.is_gt, fill=0.0, base=0,
                                                 pattern=[[0, GH], [1, P]], channel_multiplier=-1)
                ins.then_inc(masked, 1)

            def group(a, g, buf, ahead=True):
                for u in range(UNITS):
                    if a == 1 and u in MASKED_UNITS:
                        mask_probs(a, g, u)
                    if u == 3:
                        split_max(a, g, 1)
                    if u == 6 and ahead:
                        extend_v(a, g + 1, 1 - buf)
                    if u == 11 and ahead:
                        split_max(a, g + 1, 0)

            pool.memset(band[:], MASK).then_inc(area_set, 1)
            pool.wait_ge(area_set, 2)
            pool.affine_select(out=band[:], in_=band[:], compare_op=ALU.is_ge, fill=0.0, base=0,
                               pattern=[[0, 2], [1, 2 * P]], channel_multiplier=-1).then_inc(area_set, 1)
            pool.wait_ge(area_set, 3)
            pool.affine_select(out=band[:], in_=band[:], compare_op=ALU.is_gt, fill=0.0, base=WINDOW,
                               pattern=[[0, 2], [-1, 2 * P]], channel_multiplier=1).then_inc(area_set, 1)
            pool.wait_ge(area_set, 4)
            pool.memset(band[:, 0, 0:P], 0.0)
            for a in range(2):
                if a == 1:
                    pool.wait_ge(o_ready, 8)
                pool.memset(area[:, q_max_at:q_max_end], 0.0)
                if a == 1:
                    pool.wait_ge(down_ready, 8)
                pool.memset(area[:, ones_at:vaug_at], TWO_ONES).then_inc(area_set, 1)
                pool.memset(area[:, vaug_at:q_st_at], 1.0)
                if a == 0:
                    pool.wait_ge(bias_loaded, 64)
                    pool.wait_ge(ln_xn, BATCH * BT)
                    pool.tensor_tensor(x[:], x[:], bo_rows[:].rearrange("p (o d) -> p o d", o=1).to_broadcast(
                        (P, TILES, D)), ALU.add).then_inc(x_biased, 1)
                for i in range(4):
                    pool.wait_ge(stacks_stored[i], stored(i, QBASE[a] + BATCH * NQ[a]))
                pool.memset(area[:, q_st_at:q_max_at], 0.0).then_inc(area_set, 1)
                extend_v(a, 0, 0)
                split_max(a, 0, 0)
                group(a, 0, 0)
                with pool.Fori(0, (GROUPS - 2) // 2) as i:
                    group(a, 2 * i + 1, 1)
                    group(a, 2 * i + 2, 0)
                group(a, GROUPS - 1, 1, ahead=False)


_INS = ["L0_attn_a_hidden_states", "L0_attn_a_Wq", "L0_attn_a_bq", "L0_attn_a_Wk", "L0_attn_a_bk", "L0_attn_a_Wv",
        "L0_attn_a_bv", "L0_attn_a_Wo", "L0_attn_a_bo", "L0_attn_b_wq", "L0_attn_b_wk", "L0_attn_b_wv",
        "L0_attn_b_wo", "L0_ffn_w_gate", "L0_ffn_w_up", "L0_ffn_w_down"]
_OUTS = [((2, 1024, 256), "float32")]


def kernel(**inputs):
    import numpy as _np
    import concourse.bacc as _bacc
    from concourse import mybir as _mybir
    from concourse.bass_utils import run_bass_kernel_spmd as _run

    nc = _bacc.Bacc("TRN2", target_bir_lowering=False, num_devices=1)
    arrays, args = {}, []
    for name in _INS:
        a = _np.ascontiguousarray(inputs[name])
        arrays[f"in_{name}_dram"] = a
        args.append(nc.dram_tensor(f"in_{name}_dram", a.shape, _mybir.dt.from_np(a.dtype), kind="ExternalInput").ap())
    for i, (shape, dtype) in enumerate(_OUTS):
        dt = _mybir.dt.from_np(_np.dtype(dtype))
        args.append(nc.dram_tensor(f"out_{i}_dram", shape, dt, kind="ExternalOutput").ap())
    hybrid_kernel(nc, *args)
    r = _run(nc, [arrays], core_ids=[0])
    return r.results[0]["out_0_dram"]
```
